# Optimizing a Trainium2 kernel written in Bass

```python
import numpy as np
import jax
import jax.numpy as jnp

def _softmax(x, axis=-1):
    return jax.nn.softmax(x, axis=axis)

def _gelu(x):
    return jax.nn.gelu(x, approximate=True)

def _silu(x):
    return jax.nn.silu(x)

def _sigmoid(x):
    return jax.nn.sigmoid(x)

def _layernorm(x, axis=-1, eps=1e-05):
    m = jnp.mean(x, axis=axis, keepdims=True)
    v = jnp.var(x, axis=axis, keepdims=True)
    return (x - m) / jnp.sqrt(v + eps)

def _scatter_add(tgt, idx, src, axis=0):
    return tgt.at[idx].add(src)

def _segment_sum(src, seg, n):
    return jax.ops.segment_sum(src, seg, n)
kernel_name = 'mk_cond_resid_d4_seqx_r4_8db887'

def setup_inputs(seed: int=0):
    np.random.seed(seed)
    _w = jnp.asarray

    def _rec_inputs():
        import jax
        import jax.numpy as jnp
        _rk = jax.random.key(seed)
        x = 7.22e-05 + 1 * jax.random.normal(jax.random.fold_in(_rk, 1), (4, 512, 256), jnp.float32)
        _lenS = 512 - jax.random.randint(jax.random.fold_in(_rk, 7), (4,), 0, max(1, 512 // 4) + 1, jnp.int32)
        _lenS2 = 512 - jax.random.randint(jax.random.fold_in(_rk, 8), (4,), 0, max(1, 512 // 4) + 1, jnp.int32)
        cond_8 = jax.random.uniform(jax.random.fold_in(_rk, 11), (4, 8), jnp.float32, 0.0, 0.999837)
        return (x, cond_8)
    x, cond_8 = _rec_inputs()

    def _L0_cond_setup():
        import jax, jax.numpy as jnp
        import numpy as np
        key = jax.random.key(seed)
        k1, k2, k3, k4, k5 = jax.random.split(key, 5)
        B, N, T, O, G = (32, 64, 256, 256, 8)
        x = jax.random.normal(k1, (B, N, T), dtype=jnp.float32)
        y = jax.random.uniform(k2, (B, G), dtype=jnp.float32)
        weight = jax.random.normal(k3, (G, O, T), dtype=jnp.float32) * (1.0 / np.sqrt(T))
        mask = jax.random.uniform(k4, (O, T), dtype=jnp.float32)
        bias = jax.random.normal(k5, (O,), dtype=jnp.float32)
        return {'x': x, 'y': y, 'weight': weight, 'mask': mask, 'bias': bias}
    _L0_cond_all = _L0_cond_setup()
    _L0_cond_in = {k: v for k, v in _L0_cond_all.items() if k in ('weight', 'mask', 'bias')}
    del _L0_cond_all

    def _L1_cond_setup():
        import jax, jax.numpy as jnp
        import numpy as np
        B, S, D = (16, 512, 256)
        E, H = (8, 512)
        key = jax.random.key(seed)
        ks = jax.random.split(key, 8)
        scale = 0.02
        x = jax.random.normal(ks[0], (B, S, D), dtype=jnp.float32)
        opcode_onehot = jax.random.uniform(ks[1], (B, E), dtype=jnp.float32)
        W_up = jax.random.normal(ks[2], (E, H, D), dtype=jnp.float32) * scale
        b_up = jnp.zeros((E, H), dtype=jnp.float32)
        W_gate = jax.random.normal(ks[3], (E, H, D), dtype=jnp.float32) * scale
        b_gate = jnp.zeros((E, H), dtype=jnp.float32)
        W_down = jax.random.normal(ks[4], (E, D, H), dtype=jnp.float32) * scale
        b_down = jnp.zeros((E, D), dtype=jnp.float32)
        return {'x': x, 'opcode_onehot': opcode_onehot, 'W_up': W_up, 'b_up': b_up, 'W_gate': W_gate, 'b_gate': b_gate, 'W_down': W_down, 'b_down': b_down}
    _L1_cond_all = _L1_cond_setup()
    _L1_cond_in = {k: v for k, v in _L1_cond_all.items() if k in ('W_up', 'b_up', 'W_gate', 'b_gate', 'W_down', 'b_down')}
    del _L1_cond_all

    def _L2_cond_setup():
        import jax, jax.numpy as jnp
        import numpy as np
        TOP_K = 2
        NUM_MOE_LAYERS = 12

        def _gemma_mlp(x, gate_w, up_w, down_w):
            g = jnp.einsum('bsh,hi->bsi', x, gate_w)
            u = jnp.einsum('bsh,hi->bsi', x, up_w)
            return jnp.einsum('bsi,ih->bsh', jax.nn.gelu(g, approximate=True) * u, down_w)
        key = jax.random.key(seed)
        ks = jax.random.split(key, 8)
        B, S, H, I, E = (32, 64, 256, 1024, 8)
        std = 0.02
        return {'x': jax.random.normal(ks[0], (B, S, H), jnp.float32), 'router_logits': jax.random.normal(ks[1], (B, E), jnp.float32), 'skill_gate': jax.random.normal(ks[2], (E, H, I), jnp.float32) * std, 'skill_up': jax.random.normal(ks[3], (E, H, I), jnp.float32) * std, 'skill_down': jax.random.normal(ks[4], (E, I, H), jnp.float32) * std, 'shared_gate': jax.random.normal(ks[5], (H, I), jnp.float32) * std, 'shared_up': jax.random.normal(ks[6], (H, I), jnp.float32) * std, 'shared_down': jax.random.normal(ks[7], (I, H), jnp.float32) * std}
    _L2_cond_all = _L2_cond_setup()
    _L2_cond_in = {k: v for k, v in _L2_cond_all.items() if k in ('skill_gate', 'skill_up', 'skill_down', 'shared_gate', 'shared_up', 'shared_down')}
    del _L2_cond_all

    def _L3_cond_setup():
        import jax, jax.numpy as jnp
        import numpy as np
        R = 16
        ALPHA = 32.0
        SCALING = ALPHA / R
        key = jax.random.key(seed)
        ks = jax.random.split(key, 6)
        B, T, C, O, E = (16, 375, 256, 256, 8)
        x = jax.random.normal(ks[0], (B, T, C), dtype=jnp.float32)
        w = jax.random.uniform(ks[1], (B, E), dtype=jnp.float32)
        W_base = jax.random.normal(ks[2], (O, C), dtype=jnp.float32) * 0.02
        b_base = jax.random.normal(ks[3], (O,), dtype=jnp.float32) * 0.02
        As = jax.random.normal(ks[4], (E, R, C), dtype=jnp.float32) * 0.02
        Bs = jax.random.normal(ks[5], (E, O, R), dtype=jnp.float32) * 0.02
        return {'x': x, 'w': w, 'W_base': W_base, 'b_base': b_base, 'As': As, 'Bs': Bs}
    _L3_cond_all = _L3_cond_setup()
    _L3_cond_in = {k: v for k, v in _L3_cond_all.items() if k in ('W_base', 'b_base', 'As', 'Bs')}
    del _L3_cond_all
    return {'x': x, 'cond_8': cond_8, 'L0_cond_weight': _L0_cond_in['weight'], 'L0_cond_mask': _L0_cond_in['mask'], 'L0_cond_bias': _L0_cond_in['bias'], 'L1_cond_W_up': _L1_cond_in['W_up'], 'L1_cond_b_up': _L1_cond_in['b_up'], 'L1_cond_W_gate': _L1_cond_in['W_gate'], 'L1_cond_b_gate': _L1_cond_in['b_gate'], 'L1_cond_W_down': _L1_cond_in['W_down'], 'L1_cond_b_down': _L1_cond_in['b_down'], 'L2_cond_skill_gate': _L2_cond_in['skill_gate'], 'L2_cond_skill_up': _L2_cond_in['skill_up'], 'L2_cond_skill_down': _L2_cond_in['skill_down'], 'L2_cond_shared_gate': _L2_cond_in['shared_gate'], 'L2_cond_shared_up': _L2_cond_in['shared_up'], 'L2_cond_shared_down': _L2_cond_in['shared_down'], 'L3_cond_W_base': _L3_cond_in['W_base'], 'L3_cond_b_base': _L3_cond_in['b_base'], 'L3_cond_As': _L3_cond_in['As'], 'L3_cond_Bs': _L3_cond_in['Bs']}

def reference(x, cond_8, L0_cond_weight, L0_cond_mask, L0_cond_bias, L1_cond_W_up, L1_cond_b_up, L1_cond_W_gate, L1_cond_b_gate, L1_cond_W_down, L1_cond_b_down, L2_cond_skill_gate, L2_cond_skill_up, L2_cond_skill_down, L2_cond_shared_gate, L2_cond_shared_up, L2_cond_shared_down, L3_cond_W_base, L3_cond_b_base, L3_cond_As, L3_cond_Bs):
    import jax
    import jax.numpy as jnp

    def _L0_cond_ref(x, y, weight, mask, bias):
        import jax, jax.numpy as jnp
        import numpy as np
        masked_w = weight * mask[None, :, :]
        w_bot = jnp.einsum('bg,got->bot', y, masked_w)
        return jnp.einsum('bnt,bot->bno', x, w_bot) + bias

    def _L1_cond_ref(x, opcode_onehot, W_up, b_up, W_gate, b_gate, W_down, b_down):
        import jax, jax.numpy as jnp
        import numpy as np
        B, S, D = (16, 512, 256)
        E, H = (8, 512)
        expert = jnp.argmax(opcode_onehot, axis=-1)
        wu, bu = (W_up[expert], b_up[expert])
        wg, bg = (W_gate[expert], b_gate[expert])
        wd, bd = (W_down[expert], b_down[expert])
        up = jnp.einsum('bsd,bhd->bsh', x, wu) + bu[:, None, :]
        gate = jnp.einsum('bsd,bhd->bsh', x, wg) + bg[:, None, :]
        hidden = jax.nn.silu(up) * gate
        out = jnp.einsum('bsh,bdh->bsd', hidden, wd) + bd[:, None, :]
        return out

    def _L2_cond_ref(x, router_logits, skill_gate, skill_up, skill_down, shared_gate, shared_up, shared_down):
        import jax, jax.numpy as jnp
        import numpy as np
        TOP_K = 2
        NUM_MOE_LAYERS = 12

        def _gemma_mlp(x, gate_w, up_w, down_w):
            g = jnp.einsum('bsh,hi->bsi', x, gate_w)
            u = jnp.einsum('bsh,hi->bsi', x, up_w)
            return jnp.einsum('bsi,ih->bsh', jax.nn.gelu(g, approximate=True) * u, down_w)
        B = x.shape[0]
        E = skill_gate.shape[0]
        rw = jax.nn.softmax(router_logits.astype(jnp.float32), axis=-1)
        w, sel = jax.lax.top_k(rw, TOP_K)
        w = w / w.sum(axis=-1, keepdims=True)
        w = w.astype(x.dtype)
        scale = 1.0 / NUM_MOE_LAYERS
        w = scale * w + (1.0 - scale) * jax.lax.stop_gradient(w)
        dense_w = jnp.zeros((B, E), x.dtype).at[jnp.arange(B)[:, None], sel].add(w)

        def step(acc, params):
            g, u, d, we = params
            return (acc + we[:, None, None] * _gemma_mlp(x, g, u, d), None)
        out, _ = jax.lax.scan(step, jnp.zeros_like(x), (skill_gate, skill_up, skill_down, dense_w.T))
        out = out + _gemma_mlp(x, shared_gate, shared_up, shared_down)
        return out

    def _L3_cond_ref(x, w, W_base, b_base, As, Bs):
        import jax, jax.numpy as jnp
        import numpy as np
        R = 16
        ALPHA = 32.0
        SCALING = ALPHA / R
        out = jnp.einsum('btc,oc->bto', x, W_base) + b_base
        h = jnp.einsum('btc,erc->bter', x, As)
        lora = jnp.einsum('bter,eor,be->bto', h, Bs, w)
        return out + lora * SCALING
    x = x + _L0_cond_ref(x, cond_8, L0_cond_weight, L0_cond_mask, L0_cond_bias)
    x = x + _L1_cond_ref(x, cond_8, L1_cond_W_up, L1_cond_b_up, L1_cond_W_gate, L1_cond_b_gate, L1_cond_W_down, L1_cond_b_down)
    x = x + _L2_cond_ref(x, cond_8, L2_cond_skill_gate, L2_cond_skill_up, L2_cond_skill_down, L2_cond_shared_gate, L2_cond_shared_up, L2_cond_shared_down)
    x = x + _L3_cond_ref(x, cond_8, L3_cond_W_base, L3_cond_b_base, L3_cond_As, L3_cond_Bs)
    return x

_drawn_inputs = setup_inputs


def setup_inputs(seed=0):
    import zlib

    import numpy as np

    out = dict(_drawn_inputs(seed))
    spreads = {'L1_cond_b_up': (0.0, 0.8), 'L1_cond_b_gate': (0.0, 0.8), 'L1_cond_b_down': (0.0, 0.1)}
    factors = {'L3_cond_b_base': 5.68}
    for name, (base, spread) in spreads.items():
        noise = np.random.default_rng([zlib.crc32(name.encode()), seed]).standard_normal(out[name].shape)
        drawn = base * np.exp(spread * noise) if base else spread * noise
        out[name] = jnp.asarray(drawn.astype(out[name].dtype))
    for name, factor in factors.items():
        out[name] = (out[name] * factor).astype(out[name].dtype)
    return out
```

```python
from contextlib import ExitStack

import numpy as np

import concourse.bass as bass
from concourse import mybir

F32 = mybir.dt.float32
F32R = mybir.dt.float32r
I32 = mybir.dt.int32
ALU = mybir.AluOpType
ACT = mybir.ActivationFunctionType
AX = mybir.AxisListType

P = 128
B, T, D = 4, 512, 256
E = 8
CB = D // P
H1, H2 = 512, 1024
TILES1, TILES2 = H1 // P, H2 // P
UNITS2 = 3
WT = 3 * D
DOWN0 = 2 * D
N1 = B * TILES1
NUNITS = B * UNITS2
RAW = 8
SPLIT = 4
AHEAD = 2
RANK = 16
LORA_SCALE = 32.0 / RANK
MOE_SCALE = 1.0 / 12
GPAIR = 2
ROUTE_OFF = -3.0e38
C_COND, C_REP, C_B0, C_B3, C_REV, NCOLS = 0, 32, 36, 38, 40, 48
BU, BG, BD, NB1 = 0, TILES1, 2 * TILES1, 2 * TILES1 + CB


def build(nc, x_d, cols_d, w0_d, mask_d, w1_d, b1_d, w2_d, base_d, lora_a_d, lora_b_d, out_d):
    ctx = ExitStack()
    with ctx:
        def sb(name, shape, dt=F32):
            return ctx.enter_context(nc.sbuf_tensor(name, shape, dt))

        def psum(name, shape):
            return ctx.enter_context(nc.psum_tensor(name, shape, F32))

        def sem(name):
            return ctx.enter_context(nc.semaphore(name))

        x = sb("x", [P, B, CB, T])
        x_hi = sb("x_hi", [P, B * CB * T], F32R)
        x_lo = sb("x_lo", [P, B * CB * T], F32R)
        act = sb("act", [P, 2, T])
        hid = sb("hid", [P, 2, T])
        hid_hi = sb("hid_hi", [P, 2, T], F32R)
        hid_lo = sb("hid_lo", [P, 2, T], F32R)
        raw = sb("raw", [P, RAW, WT])
        w_hi = sb("w_hi", [P, SPLIT, WT], F32R)
        w_lo = sb("w_lo", [P, SPLIT, WT], F32R)
        w0 = sb("w0", [P, E, CB * D])
        mask = sb("mask", [P, CB * D])
        w0_sum = sb("w0_sum", [P, B, CB * D])
        w0_term = sb("w0_term", [P, CB * D])
        w0_masked = sb("w0_masked", [P, CB * D])
        w0_hi = sb("w0_hi", [P, CB * D], F32R)
        w0_lo = sb("w0_lo", [P, CB * D], F32R)
        base = sb("base", [P, CB * D])
        lora_a = sb("lora_a", [P, D])
        lora_b = sb("lora_b", [P, D])
        lora_bw = sb("lora_bw", [P, 2, D])
        w3 = sb("w3", [P, 2, CB * D])
        w3_hi = sb("w3_hi", [P, B, CB * D], F32R)
        w3_lo = sb("w3_lo", [P, B, CB * D], F32R)
        cols = sb("cols", [P, NCOLS])
        b1 = sb("b1", [P, B, NB1])
        r_eq = sb("r_eq", [P, B, E])
        r_rank = sb("r_rank", [P, B, E])
        r_one = sb("r_one", [P, 2, B, E])
        r_cond2 = sb("r_cond2", [P, B, E])
        r_exp = sb("r_exp", [P, B, E])
        r_prob = sb("r_prob", [P, B, E])
        r_max = sb("r_max", [P, 2, B])
        r_pick = sb("r_pick", [P, 2, B])
        r_sum = sb("r_sum", [P, B])
        r_inv = sb("r_inv", [P, B])
        r_two = sb("r_two", [P, 2, B])
        r_tot = sb("r_tot", [P, B])
        r_w = sb("r_w", [P, B, UNITS2])
        r_w12 = sb("r_w12", [P, B, UNITS2])
        unit_w = sb("unit_w", [P, B, UNITS2])
        expert_f = sb("expert_f", [P, B, UNITS2])
        expert = sb("expert", [P, NUNITS], I32)

        act_ps = psum("act_ps", [P, 2, T])
        lin_ps = psum("lin_ps", [P, 2, T])
        acc_ps = psum("acc_ps", [P, CB, T])
        aux_ps = psum("aux_ps", [P, CB, T])

        cols_in = sem("cols_in")
        x_in = [sem(f"x_in{b}") for b in range(B)]
        w0_in = [sem(f"w0_in{g}") for g in range(E // GPAIR)]
        mask_in = sem("mask_in")
        b1_in = [sem(f"b1_in{b}") for b in range(B)]
        l3_in = sem("l3_in")
        raw_in = [sem(f"raw_in{s}") for s in range(RAW)]
        out_stored = sem("out_stored")
        route = sem("route")
        route_exp = sem("route_exp")
        expert_ready = sem("expert_ready")
        unit_w_ready = sem("unit_w_ready")
        w0_step = sem("w0_step")
        w0_pool = sem("w0_pool")
        w0_summed = sem("w0_summed")
        w0_masked_ready = sem("w0_masked_ready")
        w0_hi_ready = sem("w0_hi_ready")
        w0_lo_ready = sem("w0_lo_ready")
        l0_done = sem("l0_done")
        l0_added = sem("l0_added")
        x_hi_ready = [sem(f"x_hi_ready{layer}") for layer in range(4)]
        x_lo_ready = [sem(f"x_lo_ready{layer}") for layer in range(4)]
        w_hi_ready = sem("w_hi_ready")
        w_lo_ready = sem("w_lo_ready")
        act_done = sem("act_done")
        lin_done = sem("lin_done")
        act_ready = sem("act_ready")
        hid_ready = sem("hid_ready")
        hid_hi_ready = sem("hid_hi_ready")
        hid_lo_ready = sem("hid_lo_ready")
        down_done = sem("down_done")
        unit_added = sem("unit_added")
        lora_bw_ready = sem("lora_bw_ready")
        lora_done = sem("lora_done")
        w3_ready = sem("w3_ready")
        w3_hi_ready = sem("w3_hi_ready")
        w3_lo_ready = sem("w3_lo_ready")
        l3_done = sem("l3_done")
        l3_added = sem("l3_added")

        def x_part(t, b, c):
            if isinstance(b, int):
                return t[:, (b * CB + c) * T:(b * CB + c + 1) * T]
            return t[:, bass.ds(b * (CB * T) + c * T, T)]

        def x_row(t, b):
            if isinstance(b, int):
                return t[:, b * CB * T:(b + 1) * CB * T]
            return t[:, bass.ds(b * (CB * T), CB * T)]

        x_flat = x[:, :, :, :].rearrange("p b c t -> p (b c t)")

        def cond(b, e):
            return cols[:, C_COND + b * E + e:C_COND + b * E + e + 1]

        def tile2(k, i):
            return k * TILES2 + (N1 + i)

        L3_BANKS = [aux_ps, None, None, acc_ps]

        def l3_bank(b, m):
            if b in (1, 2):
                return (act_ps if m == 0 else lin_ps)[:, b - 1, :]
            return L3_BANKS[b][:, m, :]

        block = ctx.enter_context(nc.Block())

        @block.sync
        def _(sp):
            def load_tile(n, j, src):
                if not isinstance(n, int) or n >= RAW:
                    sp.wait_ge(w_hi_ready, n - (RAW - 1))
                    sp.wait_ge(w_lo_ready, n - (RAW - 1))
                sp.dma_start(raw[:, j, :], src).then_inc(raw_in[j], 16)

            sp.dma_start(cols[:, :], cols_d).then_inc(cols_in, 16)
            sp.dma_start(x_row(x_flat, 0), x_d[0]).then_inc(x_in[0], 16)
            for g in range(0, E, GPAIR):
                sp.dma_start(w0[:, g:g + GPAIR, :], w0_d[:, g:g + GPAIR, :]).then_inc(w0_in[g // GPAIR], 16)
            sp.dma_start(mask[:, :], mask_d).then_inc(mask_in, 16)
            sp.wait_ge(expert_ready, 1)
            for b in range(B):
                e = sp.value_load(expert[0:1, b * UNITS2:b * UNITS2 + 1], min_val=0, max_val=E - 1)
                sp.dma_start(b1[:, b, :], b1_d[bass.ds(e, 1), :, :].rearrange("a p n -> (a p) n")).then_inc(b1_in[b], 16)
                for i in range(TILES1):
                    n = b * TILES1 + i
                    load_tile(n, n % RAW, w1_d[bass.ds(e, 1), i, :, :].rearrange("a p n -> (a p) n"))
                    if n in (1, 3, 5):
                        r = (n + 1) // 2
                        sp.dma_start(x_row(x_flat, r), x_d[r]).then_inc(x_in[r], 16)
            with sp.Fori(0, NUNITS) as k:
                e = sp.value_load(expert[0:1, bass.ds(k, 1)], min_val=0, max_val=E)
                for i in range(TILES2):
                    load_tile(tile2(k, i), i, w2_d[bass.ds(e, 1), i, :, :].rearrange("a p n -> (a p) n"))
            sp.dma_start(base[:, :], base_d).then_inc(l3_in, 16)
            sp.dma_start(lora_a[:, :], lora_a_d).then_inc(l3_in, 16)
            sp.dma_start(lora_b[:, :], lora_b_d).then_inc(l3_in, 16)
            for b in range(B):
                for m in range(CB):
                    sp.wait_ge(l3_added, b * CB + m + 1)
                    sp.dma_start(out_d[b, :, m, :], x[:, b, m, :]).then_inc(out_stored, 16)
            sp.wait_ge(out_stored, 16 * B * CB)

        @block.tensor
        def _(pe):
            def product(out, hi, lo, cols_of, mov_hi, mov_lo, first, last, done=None):
                n = len(cols_of)
                for q, c in enumerate(cols_of):
                    pe.matmul(out, hi[:, c:c + P], mov_hi[q], start=first and q == 0, stop=False)
                    pe.matmul(out, hi[:, c:c + P], mov_lo[q], start=False, stop=False)
                    mm = pe.matmul(out, lo[:, c:c + P], mov_hi[q], start=False, stop=last and q == n - 1)
                if done is not None:
                    mm.then_inc(done, 1)

            def up(n, j, xh, xl):
                hi, lo = w_hi[:, j % SPLIT, :], w_lo[:, j % SPLIT, :]
                pe.wait_ge(w_hi_ready, n + 1)
                pe.wait_ge(w_lo_ready, n + 1)
                if not isinstance(n, int) or n >= 2:
                    pe.wait_ge(act_ready, n - 1)
                product(act_ps[:, j % 2, :], hi, lo, [c * P for c in range(CB)], xh, xl, True, True, act_done)
                if not isinstance(n, int) or n >= 2:
                    pe.wait_ge(hid_ready, n - 1)
                product(lin_ps[:, j % 2, :], hi, lo, [D + c * P for c in range(CB)], xh, xl, True, True, lin_done)

            def down(n, j, first, last, unit):
                pe.wait_ge(hid_lo_ready, n + 1)
                if first and not (isinstance(unit, int) and unit == 0):
                    pe.wait_ge(unit_added, unit)
                hi, lo = w_hi[:, j % SPLIT, :], w_lo[:, j % SPLIT, :]
                for m in range(CB):
                    product(acc_ps[:, m, :], hi, lo, [DOWN0 + m * P], [hid_hi[:, j % 2, :]], [hid_lo[:, j % 2, :]],
                            first, last, down_done if m == CB - 1 else None)

            def x_parts(b):
                return [x_part(x_hi, b, c) for c in range(CB)], [x_part(x_lo, b, c) for c in range(CB)]

            def layer0(b):
                pe.wait_ge(x_hi_ready[0], b + 1)
                pe.wait_ge(x_lo_ready[0], b + 1)
                pe.wait_ge(w0_hi_ready, b + 1)
                pe.wait_ge(w0_lo_ready, b + 1)
                if b >= 1:
                    pe.wait_ge(l0_added, b)
                xh, xl = x_parts(b)
                for m in range(CB):
                    product(aux_ps[:, m, :], w0_hi[:, :], w0_lo[:, :], [c * D + m * P for c in range(CB)],
                            xh, xl, True, True, l0_done if m == CB - 1 else None)

            def lora(b):
                if b == 0:
                    pe.wait_ge(l3_in, 48)
                    pe.wait_ge(l0_added, B)
                else:
                    pe.wait_ge(w3_ready, b)
                pe.wait_ge(lora_bw_ready, b + 1)
                for c in range(CB):
                    mm = pe.matmul(aux_ps[:, 0, c * D:(c + 1) * D], lora_a[:, c * P:(c + 1) * P],
                                   lora_bw[:, b % 2, :], start=True, stop=True)
                mm.then_inc(lora_done, 1)

            def layer3(b):
                pe.wait_ge(x_hi_ready[3], b + 1)
                pe.wait_ge(x_lo_ready[3], b + 1)
                pe.wait_ge(w3_hi_ready, b + 1)
                pe.wait_ge(w3_lo_ready, b + 1)
                if b == B - 1:
                    pe.wait_ge(unit_added, B + NUNITS)
                xh, xl = x_parts(b)
                for m in range(CB):
                    product(l3_bank(b, m), w3_hi[:, b, :], w3_lo[:, b, :], [c * D + m * P for c in range(CB)],
                            xh, xl, True, True, l3_done)

            layer0(0)
            for n in range(N1):
                b, i = divmod(n, TILES1)
                if i == 0:
                    pe.wait_ge(x_hi_ready[1], b + 1)
                    pe.wait_ge(x_lo_ready[1], b + 1)
                up(n, n % RAW, *x_parts(b))
                if n >= 1:
                    down(n - 1, (n - 1) % RAW, (n - 1) % TILES1 == 0, i == 0, (n - 1) // TILES1)
                if i == 1 and b + 1 < B:
                    layer0(b + 1)

            def unit2(k, row, last=False):
                pe.wait_ge(x_hi_ready[2], row + 1)
                pe.wait_ge(x_lo_ready[2], row + 1)
                xh, xl = x_parts(row)
                for i in range(TILES2):
                    up(tile2(k, i), i, xh, xl)
                    down(tile2(k, i - 1), (i - 1) % RAW, i == 1, i == 0, k + B)
                    if last and 1 <= i <= B:
                        lora(i - 1)

            with pe.Fori(0, NUNITS - 1) as k:
                unit2(k, pe.snap(k // UNITS2))
            unit2(NUNITS - 1, B - 1, last=True)
            layer3(0)
            down(tile2(NUNITS, -1), RAW - 1, False, True, None)
            for b in range(1, B):
                layer3(b)

        @block.scalar
        def _(act_e):
            def split_weights(n, j):
                act_e.wait_ge(raw_in[j], 16 * (n // RAW + 1) if isinstance(n, int) else n * 2 + (16 - 2 * j))
                if not isinstance(n, int) or n >= SPLIT:
                    act_e.wait_ge(down_done, n - (SPLIT - 1))
                act_e.activation(w_hi[:, j % SPLIT, :], raw[:, j, :], ACT.Copy).then_inc(w_hi_ready, 1)

            def activate(n, j, func, bias):
                act_e.wait_ge(act_done, n + 1)
                if not isinstance(n, int) or n >= 2:
                    act_e.wait_ge(hid_ready, n - 1)
                act_e.activation(act[:, j % 2, :], act_ps[:, j % 2, :], func, bias=bias).then_inc(act_ready, 1)

            def split_hidden(n, j):
                act_e.wait_ge(hid_ready, n + 1)
                if not isinstance(n, int) or n >= 2:
                    act_e.wait_ge(down_done, n - 1)
                act_e.activation(hid_hi[:, j % 2, :], hid[:, j % 2, :], ACT.Copy).then_inc(hid_hi_ready, 1)

            def split_x(b, layer):
                act_e.activation(x_row(x_hi, b), x_row(x_flat, b), ACT.Copy).then_inc(x_hi_ready[layer], 1)

            def split_w0(b):
                act_e.wait_ge(w0_masked_ready, b + 1)
                if b >= 1:
                    act_e.wait_ge(l0_done, b)
                act_e.activation(w0_hi[:, :], w0_masked[:, :], ACT.Copy).then_inc(w0_hi_ready, 1)

            act_e.wait_ge(route, 3)
            act_e.activation(r_exp[:, :, :], r_prob[:, :, :], ACT.Exp).then_inc(route_exp, 1)
            act_e.wait_ge(x_in[0], 16)
            split_x(0, 0)
            split_weights(0, 0)
            split_w0(0)
            split_weights(1, 1)
            act_e.wait_ge(l0_added, 1)
            split_x(0, 1)
            for n in range(N1):
                b, i = divmod(n, TILES1)
                if i == 0:
                    act_e.wait_ge(b1_in[b], 16)
                activate(n, n % RAW, ACT.Silu, b1[:, b, BU + i:BU + i + 1])
                split_weights(n + AHEAD, (n + AHEAD) % RAW)
                split_hidden(n, n % RAW)
                if i == 0 and b + 1 < B:
                    split_w0(b + 1)
                    act_e.wait_ge(x_in[b + 1], 16)
                    split_x(b + 1, 0)
                if i == 1 and b >= 1:
                    act_e.wait_ge(unit_added, b)
                    split_x(b - 1, 2)
                if i == 2 and b + 1 < B:
                    act_e.wait_ge(l0_added, b + 2)
                    split_x(b + 1, 1)

            def unit2(k, first=False, last=False):
                for i in range(TILES2):
                    n = tile2(k, i)
                    activate(n, i, ACT.Gelu_apprx_tanh, 0.0)
                    if not last or i + AHEAD < TILES2:
                        split_weights(tile2(k, i + AHEAD), (i + AHEAD) % RAW)
                    split_hidden(n, i)
                    if first and i == 1:
                        act_e.wait_ge(unit_added, B)
                        split_x(B - 1, 2)
                    if last and 2 <= i < 2 + B:
                        act_e.wait_ge(w3_ready, i - 1)
                        act_e.activation(w3_hi[:, i - 2, :], w3[:, i % 2, :], ACT.Copy).then_inc(w3_hi_ready, 1)
                    if last and 3 <= i < 2 + B:
                        split_x(i - 3, 3)

            unit2(0, first=True)
            with act_e.Fori(1, NUNITS - 1) as k:
                unit2(k)
            unit2(NUNITS - 1, last=True)
            act_e.wait_ge(unit_added, B + NUNITS)
            split_x(B - 1, 3)

        @block.vector
        def _(dve):
            step = [0]

            def routed(ins):
                step[0] += 1
                ins.then_inc(route, 1)
                dve.wait_ge(route, step[0])

            c8 = cols[:, C_COND:C_COND + B * E].rearrange("p (b e) -> p b e", b=B)
            rev = cols[:, C_REV:C_REV + E].rearrange("p (a e) -> p a e", a=1).to_broadcast([P, B, E])

            def each(t):
                return t.rearrange("p (b a) -> p b a", a=1).to_broadcast([P, B, E])

            def pick(q, values):
                if q:
                    routed(dve.tensor_reduce(r_max[:, q, :], values, AX.X, ALU.max))
                routed(dve.tensor_tensor(r_eq[:, :, :], values, each(r_max[:, q, :]), ALU.is_ge))
                routed(dve.tensor_tensor(r_rank[:, :, :], r_eq[:, :, :], rev, ALU.mult))
                routed(dve.tensor_reduce(r_pick[:, q, :], r_rank[:, :, :], AX.X, ALU.max))
                routed(dve.tensor_tensor(r_one[:, q, :, :], rev, each(r_pick[:, q, :]), ALU.is_equal))

            def routing():
                dve.wait_ge(cols_in, 16)
                routed(dve.memset(expert_f[:, :, :], float(E)))
                routed(dve.tensor_reduce(r_max[:, 0, :], c8, AX.X, ALU.max))
                routed(dve.tensor_tensor(r_prob[:, :, :], c8, each(r_max[:, 0, :]), ALU.subtract))
                pick(0, c8)
                routed(dve.scalar_tensor_tensor(out=r_cond2[:, :, :].rearrange("p b e -> p (b e)"),
                                                in0=r_one[:, 0, :, :].rearrange("p b e -> p (b e)"), scalar=ROUTE_OFF,
                                                in1=cols[:, C_COND:C_COND + B * E], op0=ALU.mult, op1=ALU.add))
                pick(1, r_cond2[:, :, :])
                for q in range(2):
                    routed(dve.tensor_scalar(expert_f[:, :, q], r_pick[:, q, :], -1.0, float(E), ALU.mult, ALU.add))
                dve.tensor_copy(expert[:, :], expert_f[:, :, :].rearrange("p b u -> p (b u)")).then_inc(expert_ready, 1)

            def routing_weights():
                dve.wait_ge(route_exp, 1)
                routed(dve.tensor_reduce(r_sum[:, :], r_exp[:, :, :], AX.X, ALU.add))
                routed(dve.reciprocal(r_inv[:, :], r_sum[:, :]))
                routed(dve.tensor_tensor(r_prob[:, :, :], r_exp[:, :, :], each(r_inv[:, :]), ALU.mult))
                routed(dve.memset(unit_w[:, :, :], 1.0))
                for q in range(2):
                    routed(dve.tensor_tensor(r_rank[:, :, :], r_prob[:, :, :], r_one[:, q, :, :], ALU.mult))
                    routed(dve.tensor_reduce(r_two[:, q, :], r_rank[:, :, :], AX.X, ALU.add))
                routed(dve.tensor_tensor(r_tot[:, :], r_two[:, 0, :], r_two[:, 1, :], ALU.add))
                routed(dve.reciprocal(r_inv[:, :], r_tot[:, :]))
                for q in range(2):
                    routed(dve.tensor_tensor(r_w[:, :, q], r_two[:, q, :], r_inv[:, :], ALU.mult))
                    routed(dve.tensor_scalar(r_w12[:, :, q], r_w[:, :, q], MOE_SCALE, None, ALU.mult))
                    last = dve.scalar_tensor_tensor(out=unit_w[:, :, q], in0=r_w[:, :, q], scalar=1.0 - MOE_SCALE,
                                                    in1=r_w12[:, :, q], op0=ALU.mult, op1=ALU.add)
                last.then_inc(unit_w_ready, 1)
                dve.wait_ge(unit_w_ready, 1)

            sums = [0]

            def sum_w0(rows, gs):
                for g in gs:
                    dve.wait_ge(w0_in[g // GPAIR], 16)
                    if g >= 1:
                        dve.wait_ge(w0_step, sums[0])
                    for b in rows:
                        if g == 0:
                            ins = dve.tensor_scalar(w0_sum[:, b, :], w0[:, g, :], cond(b, g), None, ALU.mult)
                        else:
                            ins = dve.scalar_tensor_tensor(out=w0_sum[:, b, :], in0=w0[:, g, :], scalar=cond(b, g),
                                                           in1=w0_sum[:, b, :], op0=ALU.mult, op1=ALU.add)
                        sums[0] += 1
                        ins.then_inc(w0_step, 1)

            def split_w0(b):
                dve.wait_ge(w0_hi_ready, b + 1)
                dve.tensor_tensor(w0_lo[:, :], w0_masked[:, :], w0_hi[:, :].bitcast(F32),
                                  ALU.subtract).then_inc(w0_lo_ready, 1)

            def split_weights(n, j, part, parts=2):
                a, z = part * WT // parts, (part + 1) * WT // parts
                if part == 0:
                    dve.wait_ge(w_hi_ready, n + 1)
                ins = dve.tensor_tensor(w_lo[:, j % SPLIT, a:z], raw[:, j, a:z],
                                        w_hi[:, j % SPLIT, a:z].bitcast(F32), ALU.subtract)
                if part == parts - 1:
                    ins.then_inc(w_lo_ready, 1)

            def hidden(n, j, bias):
                dve.wait_ge(act_ready, n + 1)
                dve.wait_ge(lin_done, n + 1)
                if bias is None:
                    ins = dve.tensor_tensor(hid[:, j % 2, :], lin_ps[:, j % 2, :], act[:, j % 2, :], ALU.mult)
                else:
                    ins = dve.scalar_tensor_tensor(out=hid[:, j % 2, :], in0=lin_ps[:, j % 2, :], scalar=bias,
                                                   in1=act[:, j % 2, :], op0=ALU.add, op1=ALU.mult)
                ins.then_inc(hid_ready, 1)

            def split_hidden(n, j):
                dve.wait_ge(hid_hi_ready, n + 1)
                dve.tensor_tensor(hid_lo[:, j % 2, :], hid[:, j % 2, :], hid_hi[:, j % 2, :].bitcast(F32),
                                  ALU.subtract).then_inc(hid_lo_ready, 1)

            def split_x(b, layer):
                dve.wait_ge(x_hi_ready[layer], b + 1)
                dve.tensor_tensor(x_row(x_lo, b), x_row(x_flat, b), x_row(x_hi, b).bitcast(F32),
                                  ALU.subtract).then_inc(x_lo_ready[layer], 1)

            def add_l0(b):
                dve.wait_ge(l0_done, b + 1)
                for m in range(CB):
                    ins = dve.scalar_tensor_tensor(out=x[:, b, m, :], in0=aux_ps[:, m, :],
                                                   scalar=cols[:, C_B0 + m:C_B0 + m + 1], in1=x[:, b, m, :],
                                                   op0=ALU.add, op1=ALU.add)
                ins.then_inc(l0_added, 1)

            def add_l1(b):
                dve.wait_ge(down_done, (b + 1) * TILES1)
                for m in range(CB):
                    ins = dve.scalar_tensor_tensor(out=x[:, b, m, :], in0=acc_ps[:, m, :],
                                                   scalar=b1[:, b, BD + m:BD + m + 1], in1=x[:, b, m, :],
                                                   op0=ALU.add, op1=ALU.add)
                ins.then_inc(unit_added, 1)

            def add_l2(k, row):
                dve.wait_ge(down_done, tile2(k, TILES2))
                uw = unit_w[:, :, :].rearrange("p b u -> p (b u)")
                w = uw[:, k:k + 1] if isinstance(k, int) else uw[:, bass.ds(k, 1)]
                ins = dve.scalar_tensor_tensor(out=x_row(x_flat, row), in0=acc_ps[:, :, :].rearrange("p c t -> p (c t)"),
                                               scalar=w, in1=x_row(x_flat, row), op0=ALU.mult, op1=ALU.add)
                ins.then_inc(unit_added, 1)

            def add_l3(b):
                for m in range(CB):
                    dve.wait_ge(l3_done, b * CB + m + 1)
                    dve.scalar_tensor_tensor(out=x[:, b, m, :], in0=l3_bank(b, m),
                                             scalar=cols[:, C_B3 + m:C_B3 + m + 1], in1=x[:, b, m, :],
                                             op0=ALU.add, op1=ALU.add).then_inc(l3_added, 1)

            routing()
            routing_weights()
            sum_w0([0, 1], range(E))
            dve.wait_ge(mask_in, 16)
            dve.wait_ge(w0_step, sums[0])
            dve.tensor_tensor(w0_masked[:, :], w0_sum[:, 0, :], mask[:, :], ALU.mult).then_inc(w0_masked_ready, 1)
            sum_w0([2], range(1))
            split_w0(0)
            split_weights(0, 0, 0, 1)
            sum_w0([2], range(1, 4))
            add_l0(0)
            split_weights(1, 1, 0, 1)
            split_x(0, 1)
            dve.wait_ge(w0_step, sums[0])
            dve.engine_nop().then_inc(w0_summed, 1)

            for n in range(N1):
                b, i = divmod(n, TILES1)
                if i == 0:
                    dve.wait_ge(b1_in[b], 16)
                hidden(n, n % RAW, b1[:, b, BG + i:BG + i + 1])
                split_weights(n + AHEAD, (n + AHEAD) % RAW, 0)
                split_hidden(n, n % RAW)
                split_weights(n + AHEAD, (n + AHEAD) % RAW, 1)
                if i == 0 and b + 1 < B:
                    split_w0(b + 1)
                if b == 0 and i in (1, 2):
                    sum_w0([2], range(2 * i + 2, 2 * i + 4))
                if b == 0 and i == 3:
                    dve.wait_ge(w0_step, sums[0])
                    dve.engine_nop().then_inc(w0_summed, 1)
                if i == 0 and b >= 1:
                    add_l1(b - 1)
                if i == 1 and b >= 1:
                    split_x(b - 1, 2)
                if i == 2 and b + 1 < B:
                    add_l0(b + 1)
                if i == 3 and b + 1 < B:
                    split_x(b + 1, 1)

            def unit2(k, row, first=False, last=False):
                for i in range(TILES2):
                    n = tile2(k, i)
                    ahead = not last or i + AHEAD < TILES2
                    hidden(n, i, None)
                    if ahead:
                        split_weights(tile2(k, i + AHEAD), (i + AHEAD) % RAW, 0)
                    split_hidden(n, i)
                    if ahead:
                        split_weights(tile2(k, i + AHEAD), (i + AHEAD) % RAW, 1)
                    if i == 0:
                        if first:
                            add_l1(B - 1)
                        else:
                            add_l2(k - 1, row)
                    if first and i == 1:
                        split_x(B - 1, 2)
                    if last and i < B:
                        if i == 0:
                            dve.wait_ge(l3_in, 48)
                        if i >= 2:
                            dve.wait_ge(lora_done, i - 1)
                        dve.tensor_scalar(lora_bw[:, i % 2, :], lora_b[:, :], cols[:, C_REP + i:C_REP + i + 1],
                                          LORA_SCALE, ALU.mult, ALU.mult).then_inc(lora_bw_ready, 1)
                    if last and 2 <= i < 2 + B:
                        b = i - 2
                        dve.wait_ge(lora_done, b + 1)
                        if b >= 2:
                            dve.wait_ge(w3_hi_ready, b - 1)
                        dve.tensor_tensor(w3[:, i % 2, :], aux_ps[:, 0, :], base[:, :], ALU.add).then_inc(w3_ready, 1)
                    if last and 3 <= i < 3 + B:
                        b = i - 3
                        dve.wait_ge(w3_hi_ready, b + 1)
                        dve.tensor_tensor(w3_lo[:, b, :], w3[:, b % 2, :], w3_hi[:, b, :].bitcast(F32),
                                          ALU.subtract).then_inc(w3_lo_ready, 1)
                    if last and 4 <= i < 3 + B:
                        split_x(i - 4, 3)

            unit2(0, None, first=True)
            with dve.Fori(1, NUNITS - 1) as k:
                unit2(k, dve.snap((k - 1) // UNITS2))
            unit2(NUNITS - 1, B - 1, last=True)
            dve.wait_ge(w3_hi_ready, B)
            add_l2(NUNITS - 1, B - 1)
            add_l3(0)
            split_x(B - 1, 3)
            for b in range(1, B):
                add_l3(b)

        @block.gpsimd
        def _(pool):
            def split_x(b):
                pool.wait_ge(x_hi_ready[0], b + 1)
                pool.tensor_tensor(x_row(x_lo, b), x_row(x_flat, b), x_row(x_hi, b).bitcast(F32),
                                   ALU.subtract).then_inc(x_lo_ready[0], 1)

            def mask_w0(b):
                pool.wait_ge(w0_lo_ready, b)
                pool.tensor_tensor(w0_masked[:, :], w0_sum[:, b, :], mask[:, :],
                                   ALU.mult).then_inc(w0_masked_ready, 1)

            split_x(0)
            pool.wait_ge(mask_in, 16)
            pool.wait_ge(w0_summed, 1)
            mask_w0(1)
            split_x(1)
            b, done = B - 1, 0
            for g in range(E):
                pool.wait_ge(w0_in[g // GPAIR], 16)
                if g == 0:
                    pool.wait_ge(cols_in, 16)
                dst = w0_sum[:, b, :] if g == 0 else w0_term[:, :]
                pool.tensor_scalar(dst, w0[:, g, :], cond(b, g), None, ALU.mult).then_inc(w0_pool, 1)
                done += 1
                pool.wait_ge(w0_pool, done)
                if g >= 1:
                    pool.tensor_tensor(w0_sum[:, b, :], w0_sum[:, b, :], w0_term[:, :], ALU.add).then_inc(w0_pool, 1)
                    done += 1
                    pool.wait_ge(w0_pool, done)
                if g == 4:
                    pool.wait_ge(w0_summed, 2)
                    mask_w0(2)
                    split_x(2)
            mask_w0(3)
            split_x(3)


def kernel(x, cond_8, L0_cond_weight, L0_cond_mask, L0_cond_bias, L1_cond_W_up, L1_cond_b_up, L1_cond_W_gate,
           L1_cond_b_gate, L1_cond_W_down, L1_cond_b_down, L2_cond_skill_gate, L2_cond_skill_up, L2_cond_skill_down,
           L2_cond_shared_gate, L2_cond_shared_up, L2_cond_shared_down, L3_cond_W_base, L3_cond_b_base, L3_cond_As,
           L3_cond_Bs):
    import concourse.bacc as bacc
    from concourse.bass_utils import run_bass_kernel_spmd

    def arr(a):
        return np.asarray(a)

    def in_blocks(a):
        a = np.swapaxes(arr(a), -1, -2)
        a = a.reshape(*a.shape[:-2], CB, P, a.shape[-1])
        return np.swapaxes(a, -3, -2)

    def tiles(a, lin, down):
        n, _, h = a.shape
        both = [w.reshape(n, CB, P, h // P, P).transpose(0, 3, 2, 1, 4).reshape(n, h // P, P, D) for w in (a, lin)]
        return np.concatenate([*both, down.reshape(n, h // P, P, D)], axis=-1)

    def swap(a):
        return np.swapaxes(arr(a), -1, -2)

    def with_shared(skill, shared):
        return np.concatenate([arr(skill), arr(shared)[None]], axis=0)

    cond = arr(cond_8)
    cols = np.zeros((P, NCOLS), np.float32)
    cols[:, C_COND:C_COND + B * E] = cond.reshape(1, B * E)
    cols[:, C_REP:C_REP + B] = np.repeat(cond.T, RANK, axis=0)
    cols[:, C_B0:C_B0 + CB] = arr(L0_cond_bias).reshape(CB, P).T
    cols[:, C_B3:C_B3 + CB] = arr(L3_cond_b_base).reshape(CB, P).T
    cols[:, C_REV:C_REV + E] = np.arange(E, 0, -1, dtype=np.float32)

    b1 = np.concatenate([arr(L1_cond_b_up).reshape(E, TILES1, P), arr(L1_cond_b_gate).reshape(E, TILES1, P),
                         arr(L1_cond_b_down).reshape(E, CB, P)], axis=1).transpose(0, 2, 1)
    arrays = {
        "x_in": arr(x).reshape(B, T, CB, P).transpose(0, 3, 2, 1),
        "cols_in": cols,
        "w0_in": in_blocks(L0_cond_weight).transpose(1, 0, 2, 3).reshape(P, E, CB * D),
        "mask_in": in_blocks(L0_cond_mask).reshape(P, CB * D),
        "w1_in": tiles(swap(L1_cond_W_up), swap(L1_cond_W_gate), swap(L1_cond_W_down)),
        "b1_in": b1,
        "w2_in": tiles(with_shared(L2_cond_skill_gate, L2_cond_shared_gate),
                       with_shared(L2_cond_skill_up, L2_cond_shared_up),
                       with_shared(L2_cond_skill_down, L2_cond_shared_down)),
        "base_in": in_blocks(L3_cond_W_base).reshape(P, CB * D),
        "lora_a_in": arr(L3_cond_As).reshape(E * RANK, D),
        "lora_b_in": swap(L3_cond_Bs).reshape(E * RANK, D),
    }
    arrays = {name: np.ascontiguousarray(a) for name, a in arrays.items()}
    nc = bacc.Bacc("TRN2", target_bir_lowering=False, num_devices=1)
    args = [nc.dram_tensor(name, a.shape, F32, kind="ExternalInput").ap() for name, a in arrays.items()]
    out = nc.dram_tensor("out", (B, P, CB, T), F32, kind="ExternalOutput").ap()
    build(nc, *args, out)
    r = run_bass_kernel_spmd(nc, [arrays], core_ids=[0])
    return r.results[0]["out"].transpose(0, 3, 2, 1).reshape(B, T, D)
```

```python
from contextlib import ExitStack

import numpy as np

import concourse.bass as bass
from concourse import mybir

F32 = mybir.dt.float32
F32R = mybir.dt.float32r
I32 = mybir.dt.int32
BF16 = mybir.dt.bfloat16
ALU = mybir.AluOpType
ACT = mybir.ActivationFunctionType
AX = mybir.AxisListType

P = 128
B, T, D = 4, 512, 256
E = 8
CB = D // P
H1, H2 = 512, 1024
TILES1, TILES2 = H1 // P, H2 // P
UNITS2 = 3
WT = 3 * D
DOWN0 = 2 * D
N1 = B * TILES1
NUNITS = B * UNITS2
RAW = 8
SPLIT = 4
AHEAD = 2
RANK = 16
LORA_SCALE = 32.0 / RANK
MOE_SCALE = 1.0 / 12
WARMUP = 9
GPAIR = 2
ROUTE_OFF = -3.0e38
C_COND, C_REP, C_B0, C_B3, C_REV, NCOLS = 0, 32, 36, 38, 40, 48
BU, BG, BD, NB1 = 0, TILES1, 2 * TILES1, 2 * TILES1 + CB


def build(nc, x_d, cols_d, ident_d, w0_d, mask_d, w1_d, b1_d, w2_d, base_d, lora_a_d, lora_b_d, out_d):
    ctx = ExitStack()
    with ctx:
        def sb(name, shape, dt=F32):
            return ctx.enter_context(nc.sbuf_tensor(name, shape, dt))

        def psum(name, shape):
            return ctx.enter_context(nc.psum_tensor(name, shape, F32))

        def sem(name):
            return ctx.enter_context(nc.semaphore(name))

        x = sb("x", [P, B, CB, T])
        x_hi = sb("x_hi", [P, B * CB * T], F32R)
        x_lo = sb("x_lo", [P, B * CB * T], F32R)
        x0_hi = sb("x0_hi", [P, 2 * CB * T], F32R)
        x0_lo = sb("x0_lo", [P, 2 * CB * T], F32R)
        act = sb("act", [P, 2, T])
        hid = sb("hid", [P, 2, T])
        hid_hi = sb("hid_hi", [P, 2, T], F32R)
        hid_lo = sb("hid_lo", [P, 2, T], F32R)
        raw = sb("raw", [P, RAW, WT])
        w_hi = sb("w_hi", [P, SPLIT, WT], F32R)
        w_lo = sb("w_lo", [P, SPLIT, WT], F32R)
        w0 = sb("w0", [P, E, CB * D])
        mask = sb("mask", [P, CB * D])
        ident = sb("ident", [P, P])
        zeros = sb("zeros", [P, T], BF16)
        primed = sb("primed", [P, 2])
        diag = sb("diag", [P, E, P])
        w0_sum = sb("w0_sum", [P, B, CB * D])
        w0_term = sb("w0_term", [P, CB * D])
        w0_masked = sb("w0_masked", [P, CB * D])
        w0_hi = sb("w0_hi", [P, CB * D], F32R)
        w0_lo = sb("w0_lo", [P, CB * D], F32R)
        base = sb("base", [P, CB * D])
        lora_a = sb("lora_a", [P, D])
        lora_b = sb("lora_b", [P, D])
        lora_bw = sb("lora_bw", [P, B, D])
        w3 = sb("w3", [P, B, CB * D])
        w3_hi = sb("w3_hi", [P, B, CB * D], F32R)
        w3_lo = sb("w3_lo", [P, B, CB * D], F32R)
        cols = sb("cols", [P, NCOLS])
        b1 = sb("b1", [P, B, NB1])
        r_eq = sb("r_eq", [P, B, E])
        r_rank = sb("r_rank", [P, B, E])
        r_one = sb("r_one", [P, 2, B, E])
        r_cond2 = sb("r_cond2", [P, B, E])
        r_exp = sb("r_exp", [P, B, E])
        r_prob = sb("r_prob", [P, B, E])
        r_max = sb("r_max", [P, 2, B])
        r_pick = sb("r_pick", [P, 2, B])
        r_sum = sb("r_sum", [P, B])
        r_inv = sb("r_inv", [P, B])
        r_two = sb("r_two", [P, 2, B])
        r_tot = sb("r_tot", [P, B])
        r_w = sb("r_w", [P, B, UNITS2])
        r_w12 = sb("r_w12", [P, B, UNITS2])
        unit_w = sb("unit_w", [P, B, UNITS2])
        expert_f = sb("expert_f", [P, B, UNITS2])
        expert = sb("expert", [P, NUNITS], I32)

        act_ps = psum("act_ps", [P, 2, T])
        lin_ps = psum("lin_ps", [P, 2, T])
        acc_ps = psum("acc_ps", [P, CB, T])
        aux_ps = psum("aux_ps", [P, CB, T])

        cols_in = sem("cols_in")
        x_in = [sem(f"x_in{b}") for b in range(B)]
        w0_in = [sem(f"w0_in{g}") for g in range(E // GPAIR)]
        mask_in = sem("mask_in")
        b1_in = [sem(f"b1_in{b}") for b in range(B)]
        l3_in = sem("l3_in")
        raw_in = [sem(f"raw_in{s}") for s in range(RAW)]
        out_stored = sem("out_stored")
        route = sem("route")
        route_exp = sem("route_exp")
        expert_ready = sem("expert_ready")
        unit_w_ready = sem("unit_w_ready")
        ident_in = sem("ident_in")
        zeros_ready = sem("zeros_ready")
        primed_ready = sem("primed_ready")
        diag_ready = sem("diag_ready")
        w0_row0_done = sem("w0_row0_done")
        w0_step = sem("w0_step")
        w0_pool = sem("w0_pool")
        w0_masked_ready = sem("w0_masked_ready")
        w0_hi_ready = sem("w0_hi_ready")
        w0_lo_ready = sem("w0_lo_ready")
        l0_done = sem("l0_done")
        l0_added = sem("l0_added")
        x_hi_ready = [sem(f"x_hi_ready{layer}") for layer in range(4)]
        x_lo_ready = [sem(f"x_lo_ready{layer}") for layer in range(4)]
        last_hi_ready = sem("last_hi_ready")
        last_lo_ready = sem("last_lo_ready")
        w_hi_ready = sem("w_hi_ready")
        w_lo_ready = sem("w_lo_ready")
        act_done = sem("act_done")
        lin_done = sem("lin_done")
        act_ready = sem("act_ready")
        hid_ready = sem("hid_ready")
        hid_hi_ready = sem("hid_hi_ready")
        hid_lo_ready = sem("hid_lo_ready")
        down_done = sem("down_done")
        unit_added = sem("unit_added")
        last_added = sem("last_added")
        lora_bw_ready = sem("lora_bw_ready")
        lora_done = sem("lora_done")
        w3_ready = sem("w3_ready")
        w3_hi_ready = sem("w3_hi_ready")
        w3_lo_ready = sem("w3_lo_ready")
        l3_done = sem("l3_done")
        l3_added = sem("l3_added")

        def x_part(t, b, c):
            if isinstance(b, int):
                return t[:, (b * CB + c) * T:(b * CB + c + 1) * T]
            return t[:, bass.ds(b * (CB * T) + c * T, T)]

        def x_row(t, b):
            if isinstance(b, int):
                return t[:, b * CB * T:(b + 1) * CB * T]
            return t[:, bass.ds(b * (CB * T), CB * T)]

        def w0_half(t, m):
            return t.rearrange("p (c o) -> p c o", c=CB)[:, :, m * P:(m + 1) * P]

        x_flat = x[:, :, :, :].rearrange("p b c t -> p (b c t)")

        def cond(b, e):
            return cols[:, C_COND + b * E + e:C_COND + b * E + e + 1]

        def tile2(k, i):
            return k * TILES2 + (N1 + i)

        L3_BANKS = [aux_ps, None, None, acc_ps]

        def l3_bank(b, m):
            if b in (1, 2):
                return (act_ps if m == 0 else lin_ps)[:, b - 1, :]
            return L3_BANKS[b][:, m, :]

        block = ctx.enter_context(nc.Block())

        @block.sync
        def _(sp):
            def load_tile(n, j, src):
                if not isinstance(n, int) or n >= RAW:
                    sp.wait_ge(w_hi_ready, n - (RAW - 1))
                    sp.wait_ge(w_lo_ready, n - (RAW - 1))
                sp.dma_start(raw[:, j, :], src).then_inc(raw_in[j], 16)

            sp.dma_start(cols[:, :], cols_d).then_inc(cols_in, 16)
            sp.dma_start(ident[:, :], ident_d).then_inc(ident_in, 16)
            for g in range(0, E, GPAIR):
                sp.dma_start(w0[:, g:g + GPAIR, :], w0_d[:, g:g + GPAIR, :]).then_inc(w0_in[g // GPAIR], 16)
                if g == GPAIR:
                    sp.dma_start(x_row(x_flat, 0), x_d[0]).then_inc(x_in[0], 16)
                if g == E - GPAIR:
                    sp.dma_start(mask[:, :], mask_d).then_inc(mask_in, 16)
            sp.wait_ge(expert_ready, 1)
            for b in range(B):
                e = sp.value_load(expert[0:1, b * UNITS2:b * UNITS2 + 1], min_val=0, max_val=E - 1)
                sp.dma_start(b1[:, b, :], b1_d[bass.ds(e, 1), :, :].rearrange("a p n -> (a p) n")).then_inc(b1_in[b], 16)
                for i in range(TILES1):
                    n = b * TILES1 + i
                    load_tile(n, n % RAW, w1_d[bass.ds(e, 1), i, :, :].rearrange("a p n -> (a p) n"))
                    if n in (1, 3, 5):
                        r = (n + 1) // 2
                        sp.dma_start(x_row(x_flat, r), x_d[r]).then_inc(x_in[r], 16)
                    if n == RAW - 1:
                        sp.dma_start(lora_b[:, :], lora_b_d).then_inc(l3_in, 16)
                        sp.dma_start(lora_a[:, :], lora_a_d).then_inc(l3_in, 16)
                        sp.dma_start(base[:, :], base_d).then_inc(l3_in, 16)
            with sp.Fori(0, NUNITS) as k:
                e = sp.value_load(expert[0:1, bass.ds(k, 1)], min_val=0, max_val=E)
                for i in range(TILES2):
                    load_tile(tile2(k, i), i, w2_d[bass.ds(e, 1), i, :, :].rearrange("a p n -> (a p) n"))
            for b in range(B):
                for m in range(CB):
                    sp.wait_ge(l3_added, b * CB + m + 1)
                    sp.dma_start(out_d[b, :, m, :], x[:, b, m, :]).then_inc(out_stored, 16)
            sp.wait_ge(out_stored, 16 * B * CB)

        @block.tensor
        def _(pe):
            def product(out, hi, lo, cols_of, mov_hi, mov_lo, first, last, done=None, before=None):
                n = len(cols_of)
                for q, c in enumerate(cols_of):
                    if before is not None:
                        before(q)
                    pe.matmul(out, hi[:, c:c + P], mov_hi[q], start=first and q == 0, stop=False)
                    pe.matmul(out, hi[:, c:c + P], mov_lo[q], start=False, stop=False)
                    mm = pe.matmul(out, lo[:, c:c + P], mov_hi[q], start=False, stop=last and q == n - 1)
                if done is not None:
                    mm.then_inc(done, 1)

            def x_block(layer, b):
                def wait(c):
                    if (layer, b) == (3, B - 1):
                        pe.wait_ge(last_hi_ready, c + 1)
                        pe.wait_ge(last_lo_ready, c + 1)
                    else:
                        pe.wait_ge(x_hi_ready[layer], b * CB + c + 1)
                        pe.wait_ge(x_lo_ready[layer], b * CB + c + 1)
                return wait

            def up(n, j, xh, xl, before=None):
                hi, lo = w_hi[:, j % SPLIT, :], w_lo[:, j % SPLIT, :]
                pe.wait_ge(w_hi_ready, n + 1)
                pe.wait_ge(w_lo_ready, n + 1)
                if not isinstance(n, int) or n >= 2:
                    pe.wait_ge(act_ready, n - 1)
                product(act_ps[:, j % 2, :], hi, lo, [c * P for c in range(CB)], xh, xl, True, True, act_done, before)
                if not isinstance(n, int) or n >= 2:
                    pe.wait_ge(hid_ready, n - 1)
                product(lin_ps[:, j % 2, :], hi, lo, [D + c * P for c in range(CB)], xh, xl, True, True, lin_done)

            def down(n, j, first, last, unit):
                pe.wait_ge(hid_lo_ready, n + 1)
                if first and not (isinstance(unit, int) and unit == 0):
                    pe.wait_ge(unit_added, unit)
                hi, lo = w_hi[:, j % SPLIT, :], w_lo[:, j % SPLIT, :]
                for m in range(CB):
                    product(acc_ps[:, m, :], hi, lo, [DOWN0 + m * P], [hid_hi[:, j % 2, :]], [hid_lo[:, j % 2, :]],
                            first, last, down_done if m == CB - 1 else None)

            def x_parts(b, hi=x_hi, lo=x_lo):
                return [x_part(hi, b, c) for c in range(CB)], [x_part(lo, b, c) for c in range(CB)]

            def sum_row0():
                for g in range(E):
                    pe.wait_ge(w0_in[g // GPAIR], 16)
                    pe.wait_ge(diag_ready, g + 1)
                    mm = pe.matmul(acc_ps[:, 0, :], diag[:, g, :], w0[:, g, :], start=g == 0, stop=g == E - 1)
                mm.then_inc(w0_row0_done, 1)

            def layer0(b):
                xh, xl = x_parts(b % 2, x0_hi, x0_lo)
                for m in range(CB):
                    if b >= 1:
                        pe.wait_ge(l0_added, (b - 1) * CB + m + 1)
                    pe.wait_ge(w0_hi_ready, b * CB + m + 1)
                    pe.wait_ge(w0_lo_ready, b * CB + m + 1)
                    product(aux_ps[:, m, :], w0_hi[:, :], w0_lo[:, :], [c * D + m * P for c in range(CB)],
                            xh, xl, True, True, l0_done, x_block(0, b) if m == 0 else None)

            def lora(b):
                if b == 0:
                    pe.wait_ge(l3_in, 48)
                    pe.wait_ge(l0_added, B * CB)
                if b >= 2:
                    pe.wait_ge(w3_ready, b - 1)
                pe.wait_ge(lora_bw_ready, b + 1)
                for c in range(CB):
                    mm = pe.matmul(aux_ps[:, b % 2, c * D:(c + 1) * D], lora_a[:, c * P:(c + 1) * P],
                                   lora_bw[:, b, :], start=True, stop=True)
                mm.then_inc(lora_done, 1)

            def layer3(b):
                pe.wait_ge(w3_hi_ready, b + 1)
                pe.wait_ge(w3_lo_ready, b + 1)
                if b == 0:
                    pe.wait_ge(w3_ready, B)
                xh, xl = x_parts(b)
                for m in range(CB):
                    product(l3_bank(b, m), w3_hi[:, b, :], w3_lo[:, b, :], [c * D + m * P for c in range(CB)],
                            xh, xl, True, True, l3_done, x_block(3, b) if m == 0 else None)

            pe.wait_ge(zeros_ready, 1)
            for _ in range(WARMUP):
                pe.matmul(aux_ps[:, 1, :], zeros[:, 0:P], zeros[:, :], start=True, stop=True)
            sum_row0()
            layer0(0)
            for n in range(N1):
                b, i = divmod(n, TILES1)
                up(n, n % RAW, *x_parts(b), x_block(1, b) if i == 0 else None)
                if n >= 1:
                    down(n - 1, (n - 1) % RAW, (n - 1) % TILES1 == 0, i == 0, (n - 1) // TILES1)
                if i == 1 and b < B - 1:
                    layer0(b + 1)
                if b == B - 1:
                    lora(i)

            with pe.Fori(0, NUNITS) as k:
                row = pe.snap(k // UNITS2)
                pe.wait_ge(x_hi_ready[2], row * CB + CB)
                pe.wait_ge(x_lo_ready[2], row * CB + CB)
                xh, xl = x_parts(row)
                for i in range(TILES2):
                    up(tile2(k, i), i, xh, xl)
                    down(tile2(k, i - 1), (i - 1) % RAW, i == 1, i == 0, k + B)
            layer3(0)
            down(tile2(NUNITS, -1), RAW - 1, False, True, None)
            for b in range(1, B):
                layer3(b)

        @block.scalar
        def _(act_e):
            def split_weights(n, j):
                act_e.wait_ge(raw_in[j], 16 * (n // RAW + 1) if isinstance(n, int) else n * 2 + (16 - 2 * j))
                if not isinstance(n, int) or n >= SPLIT:
                    act_e.wait_ge(down_done, n - (SPLIT - 1))
                act_e.activation(w_hi[:, j % SPLIT, :], raw[:, j, :], ACT.Copy).then_inc(w_hi_ready, 1)

            def activate(n, j, func, bias):
                act_e.wait_ge(act_done, n + 1)
                if not isinstance(n, int) or n >= 2:
                    act_e.wait_ge(hid_ready, n - 1)
                act_e.activation(act[:, j % 2, :], act_ps[:, j % 2, :], func, bias=bias).then_inc(act_ready, 1)

            def split_hidden(n, j):
                act_e.wait_ge(hid_ready, n + 1)
                if not isinstance(n, int) or n >= 2:
                    act_e.wait_ge(down_done, n - 1)
                act_e.activation(hid_hi[:, j % 2, :], hid[:, j % 2, :], ACT.Copy).then_inc(hid_hi_ready, 1)

            def split_w0(b):
                for m in range(CB):
                    act_e.wait_ge(w0_masked_ready, b * CB + m + 1)
                    if b >= 1:
                        act_e.wait_ge(l0_done, b * CB)
                    act_e.activation(w0_half(w0_hi[:, :], m), w0_half(w0_masked[:, :], m),
                                     ACT.Copy).then_inc(w0_hi_ready, 1)

            def split_x0(b):
                act_e.wait_ge(x_in[b], 16)
                if b >= 2:
                    act_e.wait_ge(l0_done, (b - 1) * CB)
                act_e.activation(x_row(x0_hi, b % 2), x_row(x_flat, b), ACT.Copy).then_inc(x_hi_ready[0], CB)

            def split_x1(b):
                for c in range(CB):
                    act_e.wait_ge(l0_added, b * CB + c + 1)
                    act_e.activation(x_part(x_hi, b, c), x_part(x_flat, b, c), ACT.Copy).then_inc(x_hi_ready[1], 1)

            act_e.wait_ge(zeros_ready, 1)
            act_e.wait_ge(route, 3)
            act_e.activation(r_exp[:, :, :], r_prob[:, :, :], ACT.Exp).then_inc(route_exp, 1)
            act_e.activation(primed[:, 0:1], zeros[:, 0:1], ACT.Silu).then_inc(primed_ready, 1)
            split_x0(0)
            split_w0(0)
            split_weights(0, 0)
            split_weights(1, 1)
            split_x1(0)
            split_x0(1)
            for n in range(N1):
                b, i = divmod(n, TILES1)
                if i == 0:
                    act_e.wait_ge(b1_in[b], 16)
                activate(n, n % RAW, ACT.Silu, b1[:, b, BU + i:BU + i + 1])
                if i == 2 and b + 1 < B:
                    split_x1(b + 1)
                split_weights(n + AHEAD, (n + AHEAD) % RAW)
                split_hidden(n, n % RAW)
                if i == 0 and b + 1 < B:
                    split_w0(b + 1)
                if i == 2 and b + 2 < B:
                    split_x0(b + 2)
            act_e.activation(primed[:, 1:2], zeros[:, 1:2], ACT.Gelu_apprx_tanh).then_inc(primed_ready, 1)

            def unit2(k, last=False):
                for i in range(TILES2):
                    n = tile2(k, i)
                    activate(n, i, ACT.Gelu_apprx_tanh, 0.0)
                    if not last or i + AHEAD < TILES2:
                        split_weights(tile2(k, i + AHEAD), (i + AHEAD) % RAW)
                    split_hidden(n, i)

            with act_e.Fori(0, NUNITS - 1) as k:
                unit2(k)
            unit2(NUNITS - 1, last=True)
            for c in range(CB):
                act_e.wait_ge(last_added, c + 1)
                act_e.activation(x_part(x_hi, B - 1, c), x_part(x_flat, B - 1, c),
                                 ACT.Copy).then_inc(last_hi_ready, 1)

        @block.vector
        def _(dve):
            step = [0]

            def routed(ins):
                step[0] += 1
                ins.then_inc(route, 1)
                dve.wait_ge(route, step[0])

            c8 = cols[:, C_COND:C_COND + B * E].rearrange("p (b e) -> p b e", b=B)
            rev = cols[:, C_REV:C_REV + E].rearrange("p (a e) -> p a e", a=1).to_broadcast([P, B, E])

            def each(t):
                return t.rearrange("p (b a) -> p b a", a=1).to_broadcast([P, B, E])

            def pick(q, values):
                if q:
                    routed(dve.tensor_reduce(r_max[:, q, :], values, AX.X, ALU.max))
                routed(dve.tensor_tensor(r_eq[:, :, :], values, each(r_max[:, q, :]), ALU.is_ge))
                routed(dve.tensor_tensor(r_rank[:, :, :], r_eq[:, :, :], rev, ALU.mult))
                routed(dve.tensor_reduce(r_pick[:, q, :], r_rank[:, :, :], AX.X, ALU.max))
                routed(dve.tensor_tensor(r_one[:, q, :, :], rev, each(r_pick[:, q, :]), ALU.is_equal))

            def routing():
                dve.wait_ge(cols_in, 16)
                routed(dve.memset(expert_f[:, :, :], float(E)))
                routed(dve.tensor_reduce(r_max[:, 0, :], c8, AX.X, ALU.max))
                routed(dve.tensor_tensor(r_prob[:, :, :], c8, each(r_max[:, 0, :]), ALU.subtract))
                pick(0, c8)
                routed(dve.scalar_tensor_tensor(out=r_cond2[:, :, :].rearrange("p b e -> p (b e)"),
                                                in0=r_one[:, 0, :, :].rearrange("p b e -> p (b e)"), scalar=ROUTE_OFF,
                                                in1=cols[:, C_COND:C_COND + B * E], op0=ALU.mult, op1=ALU.add))
                pick(1, r_cond2[:, :, :])
                for q in range(2):
                    routed(dve.tensor_scalar(expert_f[:, :, q], r_pick[:, q, :], -1.0, float(E), ALU.mult, ALU.add))
                dve.tensor_copy(expert[:, :], expert_f[:, :, :].rearrange("p b u -> p (b u)")).then_inc(expert_ready, 1)

            def routing_weights():
                dve.wait_ge(route_exp, 1)
                routed(dve.tensor_reduce(r_sum[:, :], r_exp[:, :, :], AX.X, ALU.add))
                routed(dve.reciprocal(r_inv[:, :], r_sum[:, :]))
                routed(dve.tensor_tensor(r_prob[:, :, :], r_exp[:, :, :], each(r_inv[:, :]), ALU.mult))
                routed(dve.memset(unit_w[:, :, :], 1.0))
                for q in range(2):
                    routed(dve.tensor_tensor(r_rank[:, :, :], r_prob[:, :, :], r_one[:, q, :, :], ALU.mult))
                    routed(dve.tensor_reduce(r_two[:, q, :], r_rank[:, :, :], AX.X, ALU.add))
                routed(dve.tensor_tensor(r_tot[:, :], r_two[:, 0, :], r_two[:, 1, :], ALU.add))
                routed(dve.reciprocal(r_inv[:, :], r_tot[:, :]))
                for q in range(2):
                    routed(dve.tensor_tensor(r_w[:, :, q], r_two[:, q, :], r_inv[:, :], ALU.mult))
                    routed(dve.tensor_scalar(r_w12[:, :, q], r_w[:, :, q], MOE_SCALE, None, ALU.mult))
                    last = dve.scalar_tensor_tensor(out=unit_w[:, :, q], in0=r_w[:, :, q], scalar=1.0 - MOE_SCALE,
                                                    in1=r_w12[:, :, q], op0=ALU.mult, op1=ALU.add)
                last.then_inc(unit_w_ready, 1)
                dve.wait_ge(unit_w_ready, 1)

            def sum_w0(b, gs):
                for g in gs:
                    dve.wait_ge(w0_in[g // GPAIR], 16)
                    if g == 0:
                        ins = dve.tensor_scalar(w0_sum[:, b, :], w0[:, g, :], cond(b, g), None, ALU.mult)
                    else:
                        dve.wait_ge(w0_step, (b - 1) * E + g)
                        ins = dve.scalar_tensor_tensor(out=w0_sum[:, b, :], in0=w0[:, g, :], scalar=cond(b, g),
                                                       in1=w0_sum[:, b, :], op0=ALU.mult, op1=ALU.add)
                    ins.then_inc(w0_step, 1)

            def mask_row0():
                dve.wait_ge(mask_in, 16)
                dve.wait_ge(w0_row0_done, 1)
                for m in range(CB):
                    dve.tensor_tensor(w0_half(w0_masked[:, :], m), w0_half(acc_ps[:, 0, :], m), w0_half(mask[:, :], m),
                                      ALU.mult).then_inc(w0_masked_ready, 1)

            def split_w0(b):
                for m in range(CB):
                    dve.wait_ge(w0_hi_ready, b * CB + m + 1)
                    dve.tensor_tensor(w0_half(w0_lo[:, :], m), w0_half(w0_masked[:, :], m),
                                      w0_half(w0_hi[:, :].bitcast(F32), m), ALU.subtract).then_inc(w0_lo_ready, 1)

            def split_weights(n, j, part, parts=2):
                a, z = part * WT // parts, (part + 1) * WT // parts
                if part == 0:
                    dve.wait_ge(w_hi_ready, n + 1)
                ins = dve.tensor_tensor(w_lo[:, j % SPLIT, a:z], raw[:, j, a:z],
                                        w_hi[:, j % SPLIT, a:z].bitcast(F32), ALU.subtract)
                if part == parts - 1:
                    ins.then_inc(w_lo_ready, 1)

            def hidden(n, j, bias):
                dve.wait_ge(act_ready, n + 1)
                dve.wait_ge(lin_done, n + 1)
                if bias is None:
                    ins = dve.tensor_tensor(hid[:, j % 2, :], lin_ps[:, j % 2, :], act[:, j % 2, :], ALU.mult)
                else:
                    ins = dve.scalar_tensor_tensor(out=hid[:, j % 2, :], in0=lin_ps[:, j % 2, :], scalar=bias,
                                                   in1=act[:, j % 2, :], op0=ALU.add, op1=ALU.mult)
                ins.then_inc(hid_ready, 1)

            def split_hidden(n, j):
                dve.wait_ge(hid_hi_ready, n + 1)
                dve.tensor_tensor(hid_lo[:, j % 2, :], hid[:, j % 2, :], hid_hi[:, j % 2, :].bitcast(F32),
                                  ALU.subtract).then_inc(hid_lo_ready, 1)

            def split_x(b, hi_ready, lo_ready, count):
                for c in range(CB):
                    dve.wait_ge(hi_ready, count + c + 1)
                    dve.tensor_tensor(x_part(x_lo, b, c), x_part(x_flat, b, c), x_part(x_hi, b, c).bitcast(F32),
                                      ALU.subtract).then_inc(lo_ready, 1)

            def add_l0(b):
                for m in range(CB):
                    dve.wait_ge(l0_done, b * CB + m + 1)
                    dve.scalar_tensor_tensor(out=x[:, b, m, :], in0=aux_ps[:, m, :],
                                             scalar=cols[:, C_B0 + m:C_B0 + m + 1], in1=x[:, b, m, :],
                                             op0=ALU.add, op1=ALU.add).then_inc(l0_added, 1)

            def add_l1(b):
                dve.wait_ge(down_done, (b + 1) * TILES1)
                for m in range(CB):
                    ins = dve.scalar_tensor_tensor(out=x[:, b, m, :], in0=acc_ps[:, m, :],
                                                   scalar=b1[:, b, BD + m:BD + m + 1], in1=x[:, b, m, :],
                                                   op0=ALU.add, op1=ALU.add)
                ins.then_inc(unit_added, 1)

            def add_l2(k, row):
                dve.wait_ge(down_done, tile2(k, TILES2))
                uw = unit_w[:, :, :].rearrange("p b u -> p (b u)")
                w = uw[:, k:k + 1] if isinstance(k, int) else uw[:, bass.ds(k, 1)]
                ins = dve.scalar_tensor_tensor(out=x_row(x_flat, row), in0=acc_ps[:, :, :].rearrange("p c t -> p (c t)"),
                                               scalar=w, in1=x_row(x_flat, row), op0=ALU.mult, op1=ALU.add)
                ins.then_inc(unit_added, 1)

            def add_last():
                dve.wait_ge(down_done, tile2(NUNITS, 0))
                for c in range(CB):
                    dve.scalar_tensor_tensor(out=x[:, B - 1, c, :], in0=acc_ps[:, c, :],
                                             scalar=unit_w[:, B - 1, UNITS2 - 1:UNITS2], in1=x[:, B - 1, c, :],
                                             op0=ALU.mult, op1=ALU.add).then_inc(last_added, 1)

            def add_l3(b):
                for m in range(CB):
                    dve.wait_ge(l3_done, b * CB + m + 1)
                    dve.scalar_tensor_tensor(out=x[:, b, m, :], in0=l3_bank(b, m),
                                             scalar=cols[:, C_B3 + m:C_B3 + m + 1], in1=x[:, b, m, :],
                                             op0=ALU.add, op1=ALU.add).then_inc(l3_added, 1)

            def diagonals():
                dve.wait_ge(cols_in, 16)
                dve.wait_ge(ident_in, 16)
                for g in range(E):
                    dve.tensor_scalar(diag[:, g, :], ident[:, :], cond(0, g), None, ALU.mult).then_inc(diag_ready, 1)

            def base_plus_lora(b):
                dve.wait_ge(lora_done, b + 1)
                dve.tensor_tensor(w3[:, b, :], aux_ps[:, b % 2, :], base[:, :], ALU.add).then_inc(w3_ready, 1)

            def tile(n, j, bias, ahead=True, between=None):
                hidden(n, j, bias)
                if between is not None:
                    between()
                elif ahead:
                    split_weights(n + AHEAD, (j + AHEAD) % RAW, 0)
                split_hidden(n, j)
                if between is not None and ahead:
                    split_weights(n + AHEAD, (j + AHEAD) % RAW, 0)
                if ahead:
                    split_weights(n + AHEAD, (j + AHEAD) % RAW, 1)

            dve.memset(zeros[:, :], 0.0).then_inc(zeros_ready, 1)
            diagonals()
            routing()
            sum_w0(1, range(3))
            mask_row0()
            split_w0(0)
            sum_w0(1, range(3, 4))
            split_weights(0, 0, 0, 1)
            add_l0(0)
            split_x(0, x_hi_ready[1], x_lo_ready[1], 0)
            split_weights(1, 1, 0, 1)
            sum_w0(1, range(4, E))

            for n in range(N1):
                b, i = divmod(n, TILES1)
                if i == 0:
                    dve.wait_ge(b1_in[b], 16)
                if i == 2 and b + 1 < B:
                    add_l0(b + 1)
                if i == 3 and b + 1 < B:
                    split_x(b + 1, x_hi_ready[1], x_lo_ready[1], (b + 1) * CB)
                tile(n, n % RAW, b1[:, b, BG + i:BG + i + 1],
                     between=(lambda: add_l1(b - 1)) if i == 0 and b >= 1 else None)
                if i == 0 and b + 1 < B:
                    split_w0(b + 1)
                if b == 0 and i >= 1:
                    sum_w0(2, range(3 * i - 3, min(3 * i, E)))
                if n == TILES1:
                    routing_weights()
                if b == B - 1:
                    base_plus_lora(i)

            def unit2(k, row, first=False, last=False):
                for i in range(TILES2):
                    def between():
                        if first:
                            add_l1(B - 1)
                        else:
                            add_l2(k - 1, row)
                    tile(tile2(k, i), i, None, not last or i + AHEAD < TILES2, between if i == 0 else None)

            unit2(0, None, first=True)
            with dve.Fori(1, NUNITS - 1) as k:
                unit2(k, dve.snap((k - 1) // UNITS2))
            unit2(NUNITS - 1, B - 1, last=True)
            add_last()
            add_l3(0)
            split_x(B - 1, last_hi_ready, last_lo_ready, 0)
            for b in range(1, B):
                add_l3(b)

        @block.gpsimd
        def _(pool):
            def split_lo(b, layer):
                hi, lo, row = (x_hi, x_lo, b) if layer else (x0_hi, x0_lo, b % 2)
                pool.wait_ge(x_hi_ready[layer], (b + 1) * CB)
                pool.tensor_tensor(x_row(lo, row), x_row(x_flat, b), x_row(hi, row).bitcast(F32),
                                   ALU.subtract).then_inc(x_lo_ready[layer], CB)

            def split_both(b, layer):
                pool.tensor_copy(x_row(x_hi, b), x_row(x_flat, b)).then_inc(x_hi_ready[layer], CB)
                split_lo(b, layer)

            def mask_w0(b):
                pool.wait_ge(w0_lo_ready, b * CB)
                if b < B - 1:
                    pool.wait_ge(w0_step, b * E)
                for m in range(CB):
                    pool.tensor_tensor(w0_half(w0_masked[:, :], m), w0_half(w0_sum[:, b, :], m),
                                       w0_half(mask[:, :], m), ALU.mult).then_inc(w0_masked_ready, 1)

            def sum_w0(b, gs):
                for g in gs:
                    pool.wait_ge(w0_in[g // GPAIR], 16)
                    if g >= 1:
                        pool.wait_ge(w0_pool, 2 * g - 1)
                    dst = w0_sum[:, b, :] if g == 0 else w0_term[:, :]
                    pool.tensor_scalar(dst, w0[:, g, :], cond(b, g), None, ALU.mult).then_inc(w0_pool, 1)
                    if g >= 1:
                        pool.wait_ge(w0_pool, 2 * g)
                        pool.tensor_tensor(w0_sum[:, b, :], w0_sum[:, b, :], w0_term[:, :],
                                           ALU.add).then_inc(w0_pool, 1)

            pool.wait_ge(cols_in, 16)
            sum_w0(B - 1, range(1))
            split_lo(0, 0)
            sum_w0(B - 1, range(1, 3))
            pool.wait_ge(mask_in, 16)
            mask_w0(1)
            split_lo(1, 0)
            sum_w0(B - 1, range(3, E))
            mask_w0(2)
            split_lo(2, 0)
            pool.wait_ge(w0_pool, 2 * E - 1)
            mask_w0(3)
            split_lo(3, 0)
            pool.wait_ge(l3_in, 48)
            for b in range(B):
                pool.tensor_scalar(lora_bw[:, b, :], lora_b[:, :], cols[:, C_REP + b:C_REP + b + 1],
                                   LORA_SCALE, ALU.mult, ALU.mult).then_inc(lora_bw_ready, 1)
            for b in range(B):
                pool.wait_ge(unit_added, b + 1)
                split_both(b, 2)
            for b in range(B):
                pool.wait_ge(w3_ready, b + 1)
                pool.tensor_copy(w3_hi[:, b, :], w3[:, b, :]).then_inc(w3_hi_ready, 1)
                pool.wait_ge(w3_hi_ready, b + 1)
                pool.tensor_tensor(w3_lo[:, b, :], w3[:, b, :], w3_hi[:, b, :].bitcast(F32),
                                   ALU.subtract).then_inc(w3_lo_ready, 1)
            for b in range(B - 1):
                pool.wait_ge(unit_added, B + (b + 1) * UNITS2)
                split_both(b, 3)


def kernel(x, cond_8, L0_cond_weight, L0_cond_mask, L0_cond_bias, L1_cond_W_up, L1_cond_b_up, L1_cond_W_gate,
           L1_cond_b_gate, L1_cond_W_down, L1_cond_b_down, L2_cond_skill_gate, L2_cond_skill_up, L2_cond_skill_down,
           L2_cond_shared_gate, L2_cond_shared_up, L2_cond_shared_down, L3_cond_W_base, L3_cond_b_base, L3_cond_As,
           L3_cond_Bs):
    import concourse.bacc as bacc
    from concourse.bass_utils import run_bass_kernel_spmd

    def arr(a):
        return np.asarray(a)

    def in_blocks(a):
        a = np.swapaxes(arr(a), -1, -2)
        a = a.reshape(*a.shape[:-2], CB, P, a.shape[-1])
        return np.swapaxes(a, -3, -2)

    def tiles(a, lin, down):
        n, _, h = a.shape
        both = [w.reshape(n, CB, P, h // P, P).transpose(0, 3, 2, 1, 4).reshape(n, h // P, P, D) for w in (a, lin)]
        return np.concatenate([*both, down.reshape(n, h // P, P, D)], axis=-1)

    def swap(a):
        return np.swapaxes(arr(a), -1, -2)

    def with_shared(skill, shared):
        return np.concatenate([arr(skill), arr(shared)[None]], axis=0)

    cond = arr(cond_8)
    cols = np.zeros((P, NCOLS), np.float32)
    cols[:, C_COND:C_COND + B * E] = cond.reshape(1, B * E)
    cols[:, C_REP:C_REP + B] = np.repeat(cond.T, RANK, axis=0)
    cols[:, C_B0:C_B0 + CB] = arr(L0_cond_bias).reshape(CB, P).T
    cols[:, C_B3:C_B3 + CB] = arr(L3_cond_b_base).reshape(CB, P).T
    cols[:, C_REV:C_REV + E] = np.arange(E, 0, -1, dtype=np.float32)

    b1 = np.concatenate([arr(L1_cond_b_up).reshape(E, TILES1, P), arr(L1_cond_b_gate).reshape(E, TILES1, P),
                         arr(L1_cond_b_down).reshape(E, CB, P)], axis=1).transpose(0, 2, 1)
    arrays = {
        "x_in": arr(x).reshape(B, T, CB, P).transpose(0, 3, 2, 1),
        "cols_in": cols,
        "ident_in": np.eye(P, dtype=np.float32),
        "w0_in": in_blocks(L0_cond_weight).transpose(1, 0, 2, 3).reshape(P, E, CB * D),
        "mask_in": in_blocks(L0_cond_mask).reshape(P, CB * D),
        "w1_in": tiles(swap(L1_cond_W_up), swap(L1_cond_W_gate), swap(L1_cond_W_down)),
        "b1_in": b1,
        "w2_in": tiles(with_shared(L2_cond_skill_gate, L2_cond_shared_gate),
                       with_shared(L2_cond_skill_up, L2_cond_shared_up),
                       with_shared(L2_cond_skill_down, L2_cond_shared_down)),
        "base_in": in_blocks(L3_cond_W_base).reshape(P, CB * D),
        "lora_a_in": arr(L3_cond_As).reshape(E * RANK, D),
        "lora_b_in": swap(L3_cond_Bs).reshape(E * RANK, D),
    }
    arrays = {name: np.ascontiguousarray(a) for name, a in arrays.items()}
    nc = bacc.Bacc("TRN2", target_bir_lowering=False, num_devices=1)
    args = [nc.dram_tensor(name, a.shape, F32, kind="ExternalInput").ap() for name, a in arrays.items()]
    out = nc.dram_tensor("out", (B, P, CB, T), F32, kind="ExternalOutput").ap()
    build(nc, *args, out)
    r = run_bass_kernel_spmd(nc, [arrays], core_ids=[0])
    return r.results[0]["out"].transpose(0, 3, 2, 1).reshape(B, T, D)
```

```python
from contextlib import ExitStack

import numpy as np

import concourse.bass as bass
from concourse import mybir

F32 = mybir.dt.float32
F32R = mybir.dt.float32r
I32 = mybir.dt.int32
BF16 = mybir.dt.bfloat16
ALU = mybir.AluOpType
ACT = mybir.ActivationFunctionType
AX = mybir.AxisListType

P = 128
B, T, D = 4, 512, 256
E = 8
CB = D // P
H1, H2 = 512, 1024
TILES1, TILES2 = H1 // P, H2 // P
UNITS2 = 3
WT = 3 * D
DOWN0 = 2 * D
N1 = B * TILES1
NUNITS = B * UNITS2
RAW = 8
SPLIT = 4
AHEAD = 2
RANK = 16
LORA_SCALE = 32.0 / RANK
MOE_SCALE = 1.0 / 12
WARMUP = 9
PE_GS = 6
POOL_GS = (0, 1, 4, E)
ROUTE_OFF = -3.0e38
C_COND, C_REP, C_B0, C_B3, C_REV, NCOLS = 0, 32, 36, 38, 40, 48
BU, BG, BD, NB1 = 0, TILES1, 2 * TILES1, 2 * TILES1 + CB


def build(nc, x_d, cols_d, ident_d, w0_d, mask_d, w1_d, b1_d, w2_d, base_d, lora_a_d, lora_b_d, out_d):
    ctx = ExitStack()
    with ctx:
        def sb(name, shape, dt=F32):
            return ctx.enter_context(nc.sbuf_tensor(name, shape, dt))

        def psum(name, shape):
            return ctx.enter_context(nc.psum_tensor(name, shape, F32))

        def sem(name):
            return ctx.enter_context(nc.semaphore(name))

        x = sb("x", [P, B, CB, T])
        x_hi = sb("x_hi", [P, B * CB * T], F32R)
        x_lo = sb("x_lo", [P, B * CB * T], F32R)
        x0_hi = sb("x0_hi", [P, 2 * CB * T], F32R)
        x0_lo = sb("x0_lo", [P, 2 * CB * T], F32R)
        act = sb("act", [P, 2, T])
        hid = sb("hid", [P, 2, T])
        hid_hi = sb("hid_hi", [P, 2, T], F32R)
        hid_lo = sb("hid_lo", [P, 2, T], F32R)
        raw = sb("raw", [P, RAW, WT])
        w_hi = sb("w_hi", [P, SPLIT, WT], F32R)
        w_lo = sb("w_lo", [P, SPLIT, WT], F32R)
        w0 = sb("w0", [P, E, CB * D])
        mask = sb("mask", [P, CB * D])
        ident = sb("ident", [P, P])
        zeros = sb("zeros", [P, T], BF16)
        primed = sb("primed", [P, 2])
        diag = sb("diag", [P, PE_GS, P])
        w0_sum = sb("w0_sum", [P, B, CB * D])
        w0_term = sb("w0_term", [P, CB * D])
        w0_masked = sb("w0_masked", [P, CB * D])
        w0_hi = sb("w0_hi", [P, CB * D], F32R)
        w0_lo = sb("w0_lo", [P, CB * D], F32R)
        base = sb("base", [P, CB * D])
        lora_a = sb("lora_a", [P, D])
        lora_b = sb("lora_b", [P, D])
        lora_bw = sb("lora_bw", [P, B, D])
        rep_scaled = sb("rep_scaled", [P, B])
        w3 = sb("w3", [P, B * CB * D])
        w3_hi = sb("w3_hi", [P, B, CB * D], F32R)
        w3_lo = sb("w3_lo", [P, B, CB * D], F32R)
        cols = sb("cols", [P, NCOLS])
        b1 = sb("b1", [P, B, NB1])
        r_eq = sb("r_eq", [P, B, E])
        r_rank = sb("r_rank", [P, B, E])
        r_one = sb("r_one", [P, 2, B, E])
        r_cond2 = sb("r_cond2", [P, B, E])
        r_exp = sb("r_exp", [P, B, E])
        r_prob = sb("r_prob", [P, B, E])
        r_max = sb("r_max", [P, 2, B])
        r_pick = sb("r_pick", [P, 2, B])
        r_sum = sb("r_sum", [P, B])
        r_inv = sb("r_inv", [P, B])
        r_two = sb("r_two", [P, 2, B])
        r_tot = sb("r_tot", [P, B])
        r_w = sb("r_w", [P, B, UNITS2])
        r_w12 = sb("r_w12", [P, B, UNITS2])
        unit_w = sb("unit_w", [P, B, UNITS2])
        expert_f = sb("expert_f", [P, B, UNITS2])
        expert = sb("expert", [P, NUNITS], I32)

        act_ps = psum("act_ps", [P, 2, T])
        lin_ps = psum("lin_ps", [P, 2, T])
        acc_ps = psum("acc_ps", [P, CB, T])
        aux_ps = psum("aux_ps", [P, CB, T])

        cols_in = sem("cols_in")
        x_in = [sem(f"x_in{b}") for b in range(B)]
        w0_in = [sem(f"w0_in{g}") for g in range(E)]
        mask_in = sem("mask_in")
        b1_in = [sem(f"b1_in{b}") for b in range(B)]
        lora_b_in = sem("lora_b_in")
        lora_a_in = sem("lora_a_in")
        base_in = sem("base_in")
        raw_in = [sem(f"raw_in{s}") for s in range(RAW)]
        out_stored = sem("out_stored")
        route = sem("route")
        route_exp = sem("route_exp")
        expert_ready = sem("expert_ready")
        ident_in = sem("ident_in")
        zeros_ready = sem("zeros_ready")
        primed_ready = sem("primed_ready")
        diag_ready = sem("diag_ready")
        w0_row0_done = sem("w0_row0_done")
        w0_row0_step = sem("w0_row0_step")
        w0_step1 = sem("w0_step1")
        w0_step2 = sem("w0_step2")
        w0_pool1 = sem("w0_pool1")
        w0_pool2 = sem("w0_pool2")
        w0_pool3 = sem("w0_pool3")
        w0_masked_ready = sem("w0_masked_ready")
        w0_hi_ready = sem("w0_hi_ready")
        w0_lo_ready = sem("w0_lo_ready")
        l0_done = sem("l0_done")
        l0_added = sem("l0_added")
        x_hi_ready = [sem(f"x_hi_ready{layer}") for layer in range(4)]
        x_lo_ready = [sem(f"x_lo_ready{layer}") for layer in range(4)]
        last_hi_ready = sem("last_hi_ready")
        last_lo_ready = sem("last_lo_ready")
        w_hi_ready = sem("w_hi_ready")
        w_lo_ready = sem("w_lo_ready")
        act_done = sem("act_done")
        lin_done = sem("lin_done")
        act_ready = sem("act_ready")
        hid_ready = sem("hid_ready")
        hid_hi_ready = sem("hid_hi_ready")
        hid_lo_ready = sem("hid_lo_ready")
        down_done = sem("down_done")
        unit_added = sem("unit_added")
        last_added = sem("last_added")
        rep_scaled_ready = sem("rep_scaled_ready")
        lora_bw_ready = sem("lora_bw_ready")
        lora_done = sem("lora_done")
        w3_lora_ready = sem("w3_lora_ready")
        w3_ready = sem("w3_ready")
        w3_hi_ready = sem("w3_hi_ready")
        w3_lo_ready = sem("w3_lo_ready")
        l3_done = sem("l3_done")
        l3_added = sem("l3_added")

        def x_part(t, b, c):
            if isinstance(b, int):
                return t[:, (b * CB + c) * T:(b * CB + c + 1) * T]
            return t[:, bass.ds(b * (CB * T) + c * T, T)]

        def x_row(t, b):
            if isinstance(b, int):
                return t[:, b * CB * T:(b + 1) * CB * T]
            return t[:, bass.ds(b * (CB * T), CB * T)]

        def w0_half(t, m):
            return t.rearrange("p (c o) -> p c o", c=CB)[:, :, m * P:(m + 1) * P]

        x_flat = x[:, :, :, :].rearrange("p b c t -> p (b c t)")

        def cond(b, e):
            return cols[:, C_COND + b * E + e:C_COND + b * E + e + 1]

        def tile2(k, i):
            return k * TILES2 + (N1 + i)

        def lora_bank(b):
            return (act_ps if b < 2 else lin_ps)[:, b % 2, :]

        def l3_bank(b, m, t):
            if t > 0:
                return aux_ps[:, 0, :]
            if b in (1, 2):
                return (act_ps if m == 0 else lin_ps)[:, b - 1, :]
            return (aux_ps if b == 0 else acc_ps)[:, m, :]

        L3_PIECES = [(b, m, 0, T) for b in range(B) for m in range(CB)][:-1] + [
            (B - 1, CB - 1, 0, T // 2), (B - 1, CB - 1, T // 2, T // 2)]

        block = ctx.enter_context(nc.Block())

        @block.sync
        def _(sp):
            def load_tile(n, j, src):
                if not isinstance(n, int) or n >= RAW:
                    sp.wait_ge(w_hi_ready, n - (RAW - 1))
                    sp.wait_ge(w_lo_ready, n - (RAW - 1))
                sp.dma_start(raw[:, j, :], src).then_inc(raw_in[j], 16)

            sp.dma_start(cols[:, :], cols_d).then_inc(cols_in, 16)
            sp.dma_start(ident[:, :], ident_d).then_inc(ident_in, 16)
            for g in range(E):
                sp.dma_start(w0[:, g, :], w0_d[:, g, :]).then_inc(w0_in[g], 16)
                if g == 3:
                    sp.dma_start(x_row(x_flat, 0), x_d[0]).then_inc(x_in[0], 16)
            sp.dma_start(lora_b[:, :], lora_b_d).then_inc(lora_b_in, 16)
            sp.dma_start(lora_a[:, :], lora_a_d).then_inc(lora_a_in, 16)
            sp.dma_start(mask[:, :], mask_d).then_inc(mask_in, 16)
            sp.wait_ge(expert_ready, 1)
            for b in range(B):
                e = sp.value_load(expert[0:1, b * UNITS2:b * UNITS2 + 1], min_val=0, max_val=E - 1)
                sp.dma_start(b1[:, b, :], b1_d[bass.ds(e, 1), :, :].rearrange("a p n -> (a p) n")).then_inc(b1_in[b], 16)
                for i in range(TILES1):
                    n = b * TILES1 + i
                    load_tile(n, n % RAW, w1_d[bass.ds(e, 1), i, :, :].rearrange("a p n -> (a p) n"))
                    if n in (1, 3, 5):
                        r = (n + 1) // 2
                        sp.dma_start(x_row(x_flat, r), x_d[r]).then_inc(x_in[r], 16)
                    if n == RAW - 1:
                        sp.dma_start(base[:, :], base_d).then_inc(base_in, 16)
            with sp.Fori(0, NUNITS) as k:
                e = sp.value_load(expert[0:1, bass.ds(k, 1)], min_val=0, max_val=E)
                for i in range(TILES2):
                    load_tile(tile2(k, i), i, w2_d[bass.ds(e, 1), i, :, :].rearrange("a p n -> (a p) n"))
            for q, (b, m, t, count) in enumerate(L3_PIECES):
                sp.wait_ge(l3_added, q + 1)
                sp.dma_start(out_d[b, :, m, t:t + count], x[:, b, m, t:t + count]).then_inc(out_stored, 16)
            sp.wait_ge(out_stored, 16 * len(L3_PIECES))

        @block.tensor
        def _(pe):
            def product(out, hi, lo, cols_of, mov_hi, mov_lo, first, last, done=None, before=None):
                n = len(cols_of)
                for q, c in enumerate(cols_of):
                    if before is not None:
                        before(q)
                    pe.matmul(out, hi[:, c:c + P], mov_hi[q], start=first and q == 0, stop=False)
                    pe.matmul(out, hi[:, c:c + P], mov_lo[q], start=False, stop=False)
                    mm = pe.matmul(out, lo[:, c:c + P], mov_hi[q], start=False, stop=last and q == n - 1)
                if done is not None:
                    mm.then_inc(done, 1)

            def x_block(layer, b):
                def wait(c):
                    if (layer, b) == (3, B - 1):
                        pe.wait_ge(last_hi_ready, c + 1)
                        pe.wait_ge(last_lo_ready, c + 1)
                    else:
                        pe.wait_ge(x_hi_ready[layer], b * CB + c + 1)
                        pe.wait_ge(x_lo_ready[layer], b * CB + c + 1)
                return wait

            def up(n, j, xh, xl, before=None):
                hi, lo = w_hi[:, j % SPLIT, :], w_lo[:, j % SPLIT, :]
                pe.wait_ge(w_hi_ready, n + 1)
                pe.wait_ge(w_lo_ready, n + 1)
                if not isinstance(n, int) or n >= 2:
                    pe.wait_ge(act_ready, n - 1)
                product(act_ps[:, j % 2, :], hi, lo, [c * P for c in range(CB)], xh, xl, True, True, act_done, before)
                if not isinstance(n, int) or n >= 2:
                    pe.wait_ge(hid_ready, n - 1)
                else:
                    pe.wait_ge(w3_lora_ready, n + 3)
                product(lin_ps[:, j % 2, :], hi, lo, [D + c * P for c in range(CB)], xh, xl, True, True, lin_done)

            def down(n, j, first, last, unit):
                pe.wait_ge(hid_lo_ready, n + 1)
                if first and not (isinstance(unit, int) and unit == 0):
                    pe.wait_ge(unit_added, unit)
                hi, lo = w_hi[:, j % SPLIT, :], w_lo[:, j % SPLIT, :]
                for m in range(CB):
                    product(acc_ps[:, m, :], hi, lo, [DOWN0 + m * P], [hid_hi[:, j % 2, :]], [hid_lo[:, j % 2, :]],
                            first, last, down_done if m == CB - 1 else None)

            def x_parts(b, hi=x_hi, lo=x_lo):
                return [x_part(hi, b, c) for c in range(CB)], [x_part(lo, b, c) for c in range(CB)]

            def sum_row0():
                for g in range(PE_GS):
                    pe.wait_ge(w0_in[g], 16)
                    pe.wait_ge(diag_ready, g + 1)
                    mm = pe.matmul(acc_ps[:, 0, :], diag[:, g, :], w0[:, g, :], start=g == 0, stop=g == PE_GS - 1)
                mm.then_inc(w0_row0_done, 1)

            def layer0(b):
                xh, xl = x_parts(b % 2, x0_hi, x0_lo)
                for m in range(CB):
                    if b >= 1:
                        pe.wait_ge(l0_added, (b - 1) * CB + m + 1)
                    pe.wait_ge(w0_hi_ready, b * CB + m + 1)
                    pe.wait_ge(w0_lo_ready, b * CB + m + 1)
                    product(aux_ps[:, m, :], w0_hi[:, :], w0_lo[:, :], [c * D + m * P for c in range(CB)],
                            xh, xl, True, True, l0_done, x_block(0, b) if m == 0 else None)

            def lora(b):
                if b == 0:
                    pe.wait_ge(lora_a_in, 16)
                pe.wait_ge(lora_bw_ready, b + 1)
                for c in range(CB):
                    mm = pe.matmul(lora_bank(b)[:, c * D:(c + 1) * D],
                                   lora_a[:, c * P:(c + 1) * P], lora_bw[:, b, :], start=True, stop=True)
                mm.then_inc(lora_done, 1)

            def layer3(b):
                pe.wait_ge(w3_hi_ready, b + 1)
                pe.wait_ge(w3_lo_ready, b + 1)
                xh, xl = x_parts(b)
                for _, m, t, count in [piece for piece in L3_PIECES if piece[0] == b]:
                    if t > 0:
                        pe.wait_ge(l3_added, 1)
                    product(l3_bank(b, m, t)[:, t:t + count], w3_hi[:, b, :], w3_lo[:, b, :],
                            [c * D + m * P for c in range(CB)], [v[:, t:t + count] for v in xh],
                            [v[:, t:t + count] for v in xl], True, True, l3_done, x_block(3, b) if m == 0 else None)

            pe.wait_ge(zeros_ready, 1)
            for _ in range(WARMUP):
                pe.matmul(aux_ps[:, 1, :], zeros[:, 0:P], zeros[:, :], start=True, stop=True)
            sum_row0()
            lora(0)
            lora(1)
            layer0(0)
            lora(2)
            lora(3)
            for n in range(N1):
                b, i = divmod(n, TILES1)
                if n < 2:
                    pe.wait_ge(w3_lora_ready, n + 1)
                up(n, n % RAW, *x_parts(b), x_block(1, b) if i == 0 else None)
                if n >= 1:
                    down(n - 1, (n - 1) % RAW, (n - 1) % TILES1 == 0, i == 0, (n - 1) // TILES1)
                if i == 2 and b < B - 1:
                    layer0(b + 1)

            with pe.Fori(0, NUNITS) as k:
                row = pe.snap(k // UNITS2)
                pe.wait_ge(x_hi_ready[2], row * CB + CB)
                pe.wait_ge(x_lo_ready[2], row * CB + CB)
                xh, xl = x_parts(row)
                for i in range(TILES2):
                    up(tile2(k, i), i, xh, xl)
                    down(tile2(k, i - 1), (i - 1) % RAW, i == 1, i == 0, k + B)
            layer3(0)
            down(tile2(NUNITS, -1), RAW - 1, False, True, None)
            for b in range(1, B):
                layer3(b)

        @block.scalar
        def _(act_e):
            def split_weights(n, j):
                act_e.wait_ge(raw_in[j], 16 * (n // RAW + 1) if isinstance(n, int) else n * 2 + (16 - 2 * j))
                if not isinstance(n, int) or n >= SPLIT:
                    act_e.wait_ge(down_done, n - (SPLIT - 1))
                act_e.activation(w_hi[:, j % SPLIT, :], raw[:, j, :], ACT.Copy).then_inc(w_hi_ready, 1)

            def activate(n, j, func, bias):
                act_e.wait_ge(act_done, n + 1)
                if not isinstance(n, int) or n >= 2:
                    act_e.wait_ge(hid_ready, n - 1)
                act_e.activation(act[:, j % 2, :], act_ps[:, j % 2, :], func, bias=bias).then_inc(act_ready, 1)

            def split_hidden(n, j):
                act_e.wait_ge(hid_ready, n + 1)
                if not isinstance(n, int) or n >= 2:
                    act_e.wait_ge(down_done, n - 1)
                act_e.activation(hid_hi[:, j % 2, :], hid[:, j % 2, :], ACT.Copy).then_inc(hid_hi_ready, 1)

            def split_w0(b):
                for m in range(CB):
                    act_e.wait_ge(w0_masked_ready, b * CB + m + 1)
                    if b >= 1:
                        act_e.wait_ge(l0_done, b * CB)
                    act_e.activation(w0_half(w0_hi[:, :], m), w0_half(w0_masked[:, :], m),
                                     ACT.Copy).then_inc(w0_hi_ready, 1)

            def split_x0(b):
                act_e.wait_ge(x_in[b], 16)
                if b >= 2:
                    act_e.wait_ge(l0_done, (b - 1) * CB)
                act_e.activation(x_row(x0_hi, b % 2), x_row(x_flat, b), ACT.Copy).then_inc(x_hi_ready[0], CB)

            def split_x1(b):
                for c in range(CB):
                    act_e.wait_ge(l0_added, b * CB + c + 1)
                    act_e.activation(x_part(x_hi, b, c), x_part(x_flat, b, c), ACT.Copy).then_inc(x_hi_ready[1], 1)

            act_e.wait_ge(zeros_ready, 1)
            act_e.wait_ge(route, 3)
            act_e.activation(r_exp[:, :, :], r_prob[:, :, :], ACT.Exp).then_inc(route_exp, 1)
            act_e.activation(primed[:, 0:1], zeros[:, 0:1], ACT.Silu).then_inc(primed_ready, 1)

            def weigh_lora(b):
                act_e.activation(lora_bw[:, b, :], lora_b[:, :], ACT.Copy,
                                 scale=rep_scaled[:, b:b + 1]).then_inc(lora_bw_ready, 1)

            def copy_lora(b):
                act_e.wait_ge(lora_done, b + 1)
                act_e.activation(w3[:, b * CB * D:(b + 1) * CB * D], lora_bank(b), ACT.Copy).then_inc(w3_lora_ready, 1)

            split_x0(0)
            act_e.wait_ge(rep_scaled_ready, 1)
            act_e.wait_ge(lora_b_in, 16)
            weigh_lora(0)
            weigh_lora(1)
            split_w0(0)
            split_weights(0, 0)
            weigh_lora(2)
            weigh_lora(3)
            copy_lora(0)
            copy_lora(1)
            split_x1(0)
            copy_lora(2)
            split_weights(1, 1)
            copy_lora(3)
            split_x0(1)
            for n in range(N1):
                b, i = divmod(n, TILES1)
                if i == 0:
                    act_e.wait_ge(b1_in[b], 16)
                if i == 3 and b + 1 < B:
                    split_x1(b + 1)
                activate(n, n % RAW, ACT.Silu, b1[:, b, BU + i:BU + i + 1])
                split_weights(n + AHEAD, (n + AHEAD) % RAW)
                split_hidden(n, n % RAW)
                if i == 1 and b + 1 < B:
                    split_w0(b + 1)
                if i == 3 and b + 2 < B:
                    split_x0(b + 2)
            act_e.activation(primed[:, 1:2], zeros[:, 1:2], ACT.Gelu_apprx_tanh).then_inc(primed_ready, 1)

            def unit2(k, last=False):
                for i in range(TILES2):
                    n = tile2(k, i)
                    activate(n, i, ACT.Gelu_apprx_tanh, 0.0)
                    if not last or i + AHEAD < TILES2:
                        split_weights(tile2(k, i + AHEAD), (i + AHEAD) % RAW)
                    split_hidden(n, i)

            with act_e.Fori(0, NUNITS - 1) as k:
                unit2(k)
            unit2(NUNITS - 1, last=True)
            for c in range(CB):
                act_e.wait_ge(last_added, c + 1)
                act_e.activation(x_part(x_hi, B - 1, c), x_part(x_flat, B - 1, c),
                                 ACT.Copy).then_inc(last_hi_ready, 1)

        @block.vector
        def _(dve):
            step = [0]

            def routed(ins):
                step[0] += 1
                ins.then_inc(route, 1)
                dve.wait_ge(route, step[0])

            c8 = cols[:, C_COND:C_COND + B * E].rearrange("p (b e) -> p b e", b=B)
            rev = cols[:, C_REV:C_REV + E].rearrange("p (a e) -> p a e", a=1).to_broadcast([P, B, E])

            def each(t):
                return t.rearrange("p (b a) -> p b a", a=1).to_broadcast([P, B, E])

            def pick(q, values):
                if q:
                    routed(dve.tensor_reduce(r_max[:, q, :], values, AX.X, ALU.max))
                routed(dve.tensor_tensor(r_eq[:, :, :], values, each(r_max[:, q, :]), ALU.is_ge))
                routed(dve.tensor_tensor(r_rank[:, :, :], r_eq[:, :, :], rev, ALU.mult))
                routed(dve.tensor_reduce(r_pick[:, q, :], r_rank[:, :, :], AX.X, ALU.max))
                routed(dve.tensor_tensor(r_one[:, q, :, :], rev, each(r_pick[:, q, :]), ALU.is_equal))

            def routing():
                dve.wait_ge(cols_in, 16)
                routed(dve.memset(expert_f[:, :, :], float(E)))
                routed(dve.tensor_reduce(r_max[:, 0, :], c8, AX.X, ALU.max))
                routed(dve.tensor_tensor(r_prob[:, :, :], c8, each(r_max[:, 0, :]), ALU.subtract))
                pick(0, c8)
                routed(dve.scalar_tensor_tensor(out=r_cond2[:, :, :].rearrange("p b e -> p (b e)"),
                                                in0=r_one[:, 0, :, :].rearrange("p b e -> p (b e)"), scalar=ROUTE_OFF,
                                                in1=cols[:, C_COND:C_COND + B * E], op0=ALU.mult, op1=ALU.add))
                pick(1, r_cond2[:, :, :])
                for q in range(2):
                    routed(dve.tensor_scalar(expert_f[:, :, q], r_pick[:, q, :], -1.0, float(E), ALU.mult, ALU.add))
                dve.tensor_copy(expert[:, :], expert_f[:, :, :].rearrange("p b u -> p (b u)")).then_inc(expert_ready, 1)

            def routing_softmax():
                dve.wait_ge(route_exp, 1)
                routed(dve.tensor_reduce(r_sum[:, :], r_exp[:, :, :], AX.X, ALU.add))
                routed(dve.reciprocal(r_inv[:, :], r_sum[:, :]))
                routed(dve.tensor_tensor(r_prob[:, :, :], r_exp[:, :, :], each(r_inv[:, :]), ALU.mult))
                for q in range(2):
                    routed(dve.tensor_tensor(r_rank[:, :, :], r_prob[:, :, :], r_one[:, q, :, :], ALU.mult))
                    routed(dve.tensor_reduce(r_two[:, q, :], r_rank[:, :, :], AX.X, ALU.add))

            def routing_weights():
                routed(dve.memset(unit_w[:, :, :], 1.0))
                routed(dve.tensor_tensor(r_tot[:, :], r_two[:, 0, :], r_two[:, 1, :], ALU.add))
                routed(dve.reciprocal(r_inv[:, :], r_tot[:, :]))
                for q in range(2):
                    routed(dve.tensor_tensor(r_w[:, :, q], r_two[:, q, :], r_inv[:, :], ALU.mult))
                    routed(dve.tensor_scalar(r_w12[:, :, q], r_w[:, :, q], MOE_SCALE, None, ALU.mult))
                    routed(dve.scalar_tensor_tensor(out=unit_w[:, :, q], in0=r_w[:, :, q], scalar=1.0 - MOE_SCALE,
                                                    in1=r_w12[:, :, q], op0=ALU.mult, op1=ALU.add))

            def sum_w0(b, gs):
                for g in gs:
                    dve.wait_ge(w0_in[g], 16)
                    step, pools = (w0_step1, w0_pool1) if b == 1 else (w0_step2, w0_pool2)
                    if g == POOL_GS[b]:
                        dve.wait_ge(pools, 2 * g - 1)
                    else:
                        dve.wait_ge(step, g - POOL_GS[b])
                    ins = dve.scalar_tensor_tensor(out=w0_sum[:, b, :], in0=w0[:, g, :], scalar=cond(b, g),
                                                   in1=w0_sum[:, b, :], op0=ALU.mult, op1=ALU.add)
                    ins.then_inc(step, 1)

            def finish_row0():
                dve.wait_ge(w0_in[PE_GS], 16)
                dve.tensor_scalar(w0_sum[:, 0, :], w0[:, PE_GS, :], cond(0, PE_GS), None,
                                  ALU.mult).then_inc(w0_row0_step, 1)
                for g in range(PE_GS + 1, E):
                    dve.wait_ge(w0_in[g], 16)
                    dve.wait_ge(w0_row0_step, g - PE_GS)
                    dve.scalar_tensor_tensor(out=w0_sum[:, 0, :], in0=w0[:, g, :], scalar=cond(0, g),
                                             in1=w0_sum[:, 0, :], op0=ALU.mult, op1=ALU.add).then_inc(w0_row0_step, 1)
                dve.wait_ge(w0_row0_step, E - PE_GS)
                dve.wait_ge(w0_row0_done, 1)
                for m in range(CB):
                    dve.tensor_tensor(w0_half(w0_sum[:, 0, :], m), w0_half(acc_ps[:, 0, :], m),
                                      w0_half(w0_sum[:, 0, :], m), ALU.add).then_inc(w0_row0_step, 1)
                dve.wait_ge(mask_in, 16)
                for m in range(CB):
                    dve.wait_ge(w0_row0_step, E - PE_GS + m + 1)
                    dve.tensor_tensor(w0_half(w0_masked[:, :], m), w0_half(w0_sum[:, 0, :], m), w0_half(mask[:, :], m),
                                      ALU.mult).then_inc(w0_masked_ready, 1)

            def split_w0(b):
                for m in range(CB):
                    dve.wait_ge(w0_hi_ready, b * CB + m + 1)
                    dve.tensor_tensor(w0_half(w0_lo[:, :], m), w0_half(w0_masked[:, :], m),
                                      w0_half(w0_hi[:, :].bitcast(F32), m), ALU.subtract).then_inc(w0_lo_ready, 1)

            def split_weights(n, j, part, parts=2):
                a, z = part * WT // parts, (part + 1) * WT // parts
                if part == 0:
                    dve.wait_ge(w_hi_ready, n + 1)
                ins = dve.tensor_tensor(w_lo[:, j % SPLIT, a:z], raw[:, j, a:z],
                                        w_hi[:, j % SPLIT, a:z].bitcast(F32), ALU.subtract)
                if part == parts - 1:
                    ins.then_inc(w_lo_ready, 1)

            def hidden(n, j, bias):
                dve.wait_ge(act_ready, n + 1)
                dve.wait_ge(lin_done, n + 1)
                if bias is None:
                    ins = dve.tensor_tensor(hid[:, j % 2, :], lin_ps[:, j % 2, :], act[:, j % 2, :], ALU.mult)
                else:
                    ins = dve.scalar_tensor_tensor(out=hid[:, j % 2, :], in0=lin_ps[:, j % 2, :], scalar=bias,
                                                   in1=act[:, j % 2, :], op0=ALU.add, op1=ALU.mult)
                ins.then_inc(hid_ready, 1)

            def split_hidden(n, j):
                dve.wait_ge(hid_hi_ready, n + 1)
                dve.tensor_tensor(hid_lo[:, j % 2, :], hid[:, j % 2, :], hid_hi[:, j % 2, :].bitcast(F32),
                                  ALU.subtract).then_inc(hid_lo_ready, 1)

            def split_x(b, hi_ready, lo_ready, count):
                for c in range(CB):
                    dve.wait_ge(hi_ready, count + c + 1)
                    dve.tensor_tensor(x_part(x_lo, b, c), x_part(x_flat, b, c), x_part(x_hi, b, c).bitcast(F32),
                                      ALU.subtract).then_inc(lo_ready, 1)

            def add_l0(b):
                for m in range(CB):
                    dve.wait_ge(l0_done, b * CB + m + 1)
                    dve.scalar_tensor_tensor(out=x[:, b, m, :], in0=aux_ps[:, m, :],
                                             scalar=cols[:, C_B0 + m:C_B0 + m + 1], in1=x[:, b, m, :],
                                             op0=ALU.add, op1=ALU.add).then_inc(l0_added, 1)

            def add_l1(b):
                dve.wait_ge(down_done, (b + 1) * TILES1)
                for m in range(CB):
                    ins = dve.scalar_tensor_tensor(out=x[:, b, m, :], in0=acc_ps[:, m, :],
                                                   scalar=b1[:, b, BD + m:BD + m + 1], in1=x[:, b, m, :],
                                                   op0=ALU.add, op1=ALU.add)
                ins.then_inc(unit_added, 1)

            def add_l2(k, row):
                dve.wait_ge(down_done, tile2(k, TILES2))
                uw = unit_w[:, :, :].rearrange("p b u -> p (b u)")
                w = uw[:, k:k + 1] if isinstance(k, int) else uw[:, bass.ds(k, 1)]
                ins = dve.scalar_tensor_tensor(out=x_row(x_flat, row), in0=acc_ps[:, :, :].rearrange("p c t -> p (c t)"),
                                               scalar=w, in1=x_row(x_flat, row), op0=ALU.mult, op1=ALU.add)
                ins.then_inc(unit_added, 1)

            def add_last():
                dve.wait_ge(down_done, tile2(NUNITS, 0))
                for c in range(CB):
                    dve.scalar_tensor_tensor(out=x[:, B - 1, c, :], in0=acc_ps[:, c, :],
                                             scalar=unit_w[:, B - 1, UNITS2 - 1:UNITS2], in1=x[:, B - 1, c, :],
                                             op0=ALU.mult, op1=ALU.add).then_inc(last_added, 1)

            def add_l3(first, end):
                for q in range(first, end):
                    b, m, t, count = L3_PIECES[q]
                    dve.wait_ge(l3_done, q + 1)
                    dve.scalar_tensor_tensor(out=x[:, b, m, t:t + count], in0=l3_bank(b, m, t)[:, t:t + count],
                                             scalar=cols[:, C_B3 + m:C_B3 + m + 1], in1=x[:, b, m, t:t + count],
                                             op0=ALU.add, op1=ALU.add).then_inc(l3_added, 1)

            def diagonals():
                dve.wait_ge(cols_in, 16)
                dve.wait_ge(ident_in, 16)
                for g in range(PE_GS):
                    dve.tensor_scalar(diag[:, g, :], ident[:, :], cond(0, g), None, ALU.mult).then_inc(diag_ready, 1)

            def tile(n, j, bias, ahead=True, between=None):
                hidden(n, j, bias)
                if between is not None:
                    between()
                elif ahead:
                    split_weights(n + AHEAD, (j + AHEAD) % RAW, 0)
                split_hidden(n, j)
                if between is not None and ahead:
                    split_weights(n + AHEAD, (j + AHEAD) % RAW, 0)
                if ahead:
                    split_weights(n + AHEAD, (j + AHEAD) % RAW, 1)

            DVE_SUMS = {0: (1, range(6, E)), 1: (2, range(4, 5)), 2: (2, range(5, 7)), TILES1: (2, range(7, E))}

            dve.memset(zeros[:, :], 0.0).then_inc(zeros_ready, 1)
            diagonals()
            dve.tensor_scalar(rep_scaled[:, :], cols[:, C_REP:C_REP + B], LORA_SCALE, None,
                              ALU.mult).then_inc(rep_scaled_ready, 1)
            routing()
            sum_w0(1, range(1, 3))
            finish_row0()
            split_w0(0)
            sum_w0(1, range(3, 4))
            split_weights(0, 0, 0, 1)
            sum_w0(1, range(4, 5))
            add_l0(0)
            split_x(0, x_hi_ready[1], x_lo_ready[1], 0)
            split_weights(1, 1, 0, 1)
            sum_w0(1, range(5, 6))

            for n in range(N1):
                b, i = divmod(n, TILES1)
                if i == 0:
                    dve.wait_ge(b1_in[b], 16)
                if i == 3 and b + 1 < B:
                    add_l0(b + 1)
                    split_x(b + 1, x_hi_ready[1], x_lo_ready[1], (b + 1) * CB)
                tile(n, n % RAW, b1[:, b, BG + i:BG + i + 1],
                     between=(lambda: add_l1(b - 1)) if i == 0 and b >= 1 else None)
                if i == 1 and b + 1 < B:
                    split_w0(b + 1)
                if n in DVE_SUMS:
                    sum_w0(*DVE_SUMS[n])
                if b == 2 and i == 1:
                    routing_softmax()
                if b == 2 and i == 3:
                    routing_weights()

            def unit2(k, row, first=False, last=False):
                for i in range(TILES2):
                    def between():
                        if first:
                            add_l1(B - 1)
                        else:
                            add_l2(k - 1, row)
                    tile(tile2(k, i), i, None, not last or i + AHEAD < TILES2, between if i == 0 else None)

            unit2(0, None, first=True)
            with dve.Fori(1, NUNITS - 1) as k:
                unit2(k, dve.snap((k - 1) // UNITS2))
            unit2(NUNITS - 1, B - 1, last=True)
            add_l3(0, 1)
            add_last()
            add_l3(1, CB)
            split_x(B - 1, last_hi_ready, last_lo_ready, 0)
            add_l3(CB, len(L3_PIECES))

        @block.gpsimd
        def _(pool):
            def split_lo(b, layer):
                hi, lo, row = (x_hi, x_lo, b) if layer else (x0_hi, x0_lo, b % 2)
                pool.wait_ge(x_hi_ready[layer], (b + 1) * CB)
                pool.tensor_tensor(x_row(lo, row), x_row(x_flat, b), x_row(hi, row).bitcast(F32),
                                   ALU.subtract).then_inc(x_lo_ready[layer], CB)

            def split_both(b, layer):
                pool.tensor_copy(x_row(x_hi, b), x_row(x_flat, b)).then_inc(x_hi_ready[layer], CB)
                split_lo(b, layer)

            def mask_w0(b):
                pool.wait_ge(w0_lo_ready, b * CB)
                done, count = {1: (w0_step1, E - POOL_GS[1]), 2: (w0_step2, E - POOL_GS[2]), 3: (w0_pool3, 2 * E - 1)}[b]
                pool.wait_ge(done, count)
                for m in range(CB):
                    pool.tensor_tensor(w0_half(w0_masked[:, :], m), w0_half(w0_sum[:, b, :], m),
                                       w0_half(mask[:, :], m), ALU.mult).then_inc(w0_masked_ready, 1)

            def sum_w0(b, gs):
                w0_pool = [None, w0_pool1, w0_pool2, w0_pool3][b]
                for g in gs:
                    pool.wait_ge(w0_in[g], 16)
                    if g >= 1:
                        pool.wait_ge(w0_pool, 2 * g - 1)
                    dst = w0_sum[:, b, :] if g == 0 else w0_term[:, :]
                    pool.tensor_scalar(dst, w0[:, g, :], cond(b, g), None, ALU.mult).then_inc(w0_pool, 1)
                    if g >= 1:
                        pool.wait_ge(w0_pool, 2 * g)
                        pool.tensor_tensor(w0_sum[:, b, :], w0_sum[:, b, :], w0_term[:, :],
                                           ALU.add).then_inc(w0_pool, 1)

            pool.wait_ge(cols_in, 16)
            sum_w0(1, range(POOL_GS[1]))
            split_lo(0, 0)
            sum_w0(2, range(POOL_GS[2]))
            pool.wait_ge(mask_in, 16)
            split_lo(1, 0)
            mask_w0(1)
            sum_w0(B - 1, range(4))
            split_lo(2, 0)
            mask_w0(2)
            sum_w0(B - 1, range(4, E))
            split_lo(3, 0)
            mask_w0(3)
            for b in range(B):
                pool.wait_ge(unit_added, b + 1)
                split_both(b, 2)
            pool.wait_ge(base_in, 16)
            pool.wait_ge(w3_lora_ready, B)
            for b in range(B):
                w3_row = w3[:, b * CB * D:(b + 1) * CB * D]
                pool.tensor_tensor(w3_row, w3_row, base[:, :], ALU.add).then_inc(w3_ready, 1)
                pool.wait_ge(w3_ready, b + 1)
                pool.tensor_copy(w3_hi[:, b, :], w3_row).then_inc(w3_hi_ready, 1)
                pool.wait_ge(w3_hi_ready, b + 1)
                pool.tensor_tensor(w3_lo[:, b, :], w3_row, w3_hi[:, b, :].bitcast(F32),
                                   ALU.subtract).then_inc(w3_lo_ready, 1)
            for b in range(B - 1):
                pool.wait_ge(unit_added, B + (b + 1) * UNITS2)
                split_both(b, 3)


def kernel(x, cond_8, L0_cond_weight, L0_cond_mask, L0_cond_bias, L1_cond_W_up, L1_cond_b_up, L1_cond_W_gate,
           L1_cond_b_gate, L1_cond_W_down, L1_cond_b_down, L2_cond_skill_gate, L2_cond_skill_up, L2_cond_skill_down,
           L2_cond_shared_gate, L2_cond_shared_up, L2_cond_shared_down, L3_cond_W_base, L3_cond_b_base, L3_cond_As,
           L3_cond_Bs):
    import concourse.bacc as bacc
    from concourse.bass_utils import run_bass_kernel_spmd

    def arr(a):
        return np.asarray(a)

    def in_blocks(a):
        a = np.swapaxes(arr(a), -1, -2)
        a = a.reshape(*a.shape[:-2], CB, P, a.shape[-1])
        return np.swapaxes(a, -3, -2)

    def tiles(a, lin, down):
        n, _, h = a.shape
        both = [w.reshape(n, CB, P, h // P, P).transpose(0, 3, 2, 1, 4).reshape(n, h // P, P, D) for w in (a, lin)]
        return np.concatenate([*both, down.reshape(n, h // P, P, D)], axis=-1)

    def swap(a):
        return np.swapaxes(arr(a), -1, -2)

    def with_shared(skill, shared):
        return np.concatenate([arr(skill), arr(shared)[None]], axis=0)

    cond = arr(cond_8)
    cols = np.zeros((P, NCOLS), np.float32)
    cols[:, C_COND:C_COND + B * E] = cond.reshape(1, B * E)
    cols[:, C_REP:C_REP + B] = np.repeat(cond.T, RANK, axis=0)
    cols[:, C_B0:C_B0 + CB] = arr(L0_cond_bias).reshape(CB, P).T
    cols[:, C_B3:C_B3 + CB] = arr(L3_cond_b_base).reshape(CB, P).T
    cols[:, C_REV:C_REV + E] = np.arange(E, 0, -1, dtype=np.float32)

    b1 = np.concatenate([arr(L1_cond_b_up).reshape(E, TILES1, P), arr(L1_cond_b_gate).reshape(E, TILES1, P),
                         arr(L1_cond_b_down).reshape(E, CB, P)], axis=1).transpose(0, 2, 1)
    arrays = {
        "x_in": arr(x).reshape(B, T, CB, P).transpose(0, 3, 2, 1),
        "cols_in": cols,
        "ident_in": np.eye(P, dtype=np.float32),
        "w0_in": in_blocks(L0_cond_weight).transpose(1, 0, 2, 3).reshape(P, E, CB * D),
        "mask_in": in_blocks(L0_cond_mask).reshape(P, CB * D),
        "w1_in": tiles(swap(L1_cond_W_up), swap(L1_cond_W_gate), swap(L1_cond_W_down)),
        "b1_in": b1,
        "w2_in": tiles(with_shared(L2_cond_skill_gate, L2_cond_shared_gate),
                       with_shared(L2_cond_skill_up, L2_cond_shared_up),
                       with_shared(L2_cond_skill_down, L2_cond_shared_down)),
        "base_in": in_blocks(L3_cond_W_base).reshape(P, CB * D),
        "lora_a_in": arr(L3_cond_As).reshape(E * RANK, D),
        "lora_b_in": swap(L3_cond_Bs).reshape(E * RANK, D),
    }
    arrays = {name: np.ascontiguousarray(a) for name, a in arrays.items()}
    nc = bacc.Bacc("TRN2", target_bir_lowering=False, num_devices=1)
    args = [nc.dram_tensor(name, a.shape, F32, kind="ExternalInput").ap() for name, a in arrays.items()]
    out = nc.dram_tensor("out", (B, P, CB, T), F32, kind="ExternalOutput").ap()
    build(nc, *args, out)
    r = run_bass_kernel_spmd(nc, [arrays], core_ids=[0])
    return r.results[0]["out"].transpose(0, 3, 2, 1).reshape(B, T, D)
```
